# Optimizing a Trainium2 kernel written in Bass

```python
import numpy as np
import jax
import jax.numpy as jnp

def _softmax(x, axis=-1):
    return jax.nn.softmax(x, axis=axis)

def _gelu(x):
    return jax.nn.gelu(x, approximate=True)

def _silu(x):
    return jax.nn.silu(x)

def _sigmoid(x):
    return jax.nn.sigmoid(x)

def _layernorm(x, axis=-1, eps=1e-05):
    m = jnp.mean(x, axis=axis, keepdims=True)
    v = jnp.var(x, axis=axis, keepdims=True)
    return (x - m) / jnp.sqrt(v + eps)

def _scatter_add(tgt, idx, src, axis=0):
    return tgt.at[idx].add(src)

def _segment_sum(src, seg, n):
    return jax.ops.segment_sum(src, seg, n)
kernel_name = 'mk_xattn_seq_d2_seqx_r4_add196'

def setup_inputs(seed: int=0):
    np.random.seed(seed)
    _w = jnp.asarray

    def _rec_inputs():
        import jax
        import jax.numpy as jnp
        _rk = jax.random.key(seed)
        x = -0.0001108 + 0.9999 * jax.random.normal(jax.random.fold_in(_rk, 1), (8, 256, 320), jnp.float32)
        _lenS = 256 - jax.random.randint(jax.random.fold_in(_rk, 7), (8,), 0, max(1, 256 // 4) + 1, jnp.int32)
        _lenS2 = 256 - jax.random.randint(jax.random.fold_in(_rk, 8), (8,), 0, max(1, 256 // 4) + 1, jnp.int32)
        _ctx_2048P = jax.random.normal(jax.random.fold_in(_rk, 11), (8, 16, 512), jnp.float32)
        _ctx_2048c = jax.random.dirichlet(jax.random.fold_in(_rk, 511), 0.3 * jnp.ones((16,), jnp.float32), (8, 256))
        _ctx_2048t = jnp.einsum('bsk,bkd->bsd', _ctx_2048c, _ctx_2048P)
        _ctx_2048t = _ctx_2048t * jax.lax.rsqrt(jnp.mean(jnp.square(_ctx_2048t)) + 1e-12) * 0.953939
        ctx_2048 = -0.000395056 + 1.00006 * (_ctx_2048t + 0.3 * jax.random.normal(jax.random.fold_in(_rk, 611), (8, 256, 512), jnp.float32))
        fside_S_0 = jax.random.uniform(jax.random.fold_in(_rk, 12), (256,), jnp.float32, 0.0, 0.999706)
        return (x, ctx_2048, fside_S_0)
    x, ctx_2048, fside_S_0 = _rec_inputs()

    def _L0_xattn_setup():
        import jax, jax.numpy as jnp
        import numpy as np
        NUM_HEADS = 20
        TEXT_LEN = 77
        IP_SCALE = 1.0

        def _attend(q, k, v, sm_scale):
            scores = jnp.einsum('bhsd,bhld->bhsl', q, k) * sm_scale
            probs = jax.nn.softmax(scores, axis=-1)
            return jnp.einsum('bhsl,bhld->bhsd', probs, v)

        def _split_heads(x, h):
            b, s, c = x.shape
            return x.reshape(b, s, h, c // h).transpose(0, 2, 1, 3)

        def _merge_heads(x):
            b, h, s, d = x.shape
            return x.transpose(0, 2, 1, 3).reshape(b, s, h * d)
        key = jax.random.key(seed)
        ks = jax.random.split(key, 8)
        B, S, C, CC, L = (8, 1024, 320, 512, TEXT_LEN + 4)
        sd_q = 1.0 / np.sqrt(C)
        sd_kv = 1.0 / np.sqrt(CC)
        return {'hidden_states': jax.random.normal(ks[0], (B, S, C), jnp.float32), 'encoder_hidden_states': jax.random.normal(ks[1], (B, L, CC), jnp.float32), 'Wq': jax.random.normal(ks[2], (C, C), jnp.float32) * sd_q, 'Wk': jax.random.normal(ks[3], (C, CC), jnp.float32) * sd_kv, 'Wv': jax.random.normal(ks[4], (C, CC), jnp.float32) * sd_kv, 'Wk_ip': jax.random.normal(ks[5], (C, CC), jnp.float32) * sd_kv, 'Wv_ip': jax.random.normal(ks[6], (C, CC), jnp.float32) * sd_kv, 'Wo': jax.random.normal(ks[7], (C, C), jnp.float32) * sd_q, 'bo': jnp.zeros((C,), jnp.float32)}
    _L0_xattn_all = _L0_xattn_setup()
    _L0_xattn_in = {k: v for k, v in _L0_xattn_all.items() if k in ('Wq', 'Wk', 'Wv', 'Wk_ip', 'Wv_ip', 'Wo', 'bo')}
    del _L0_xattn_all

    def _L1_xattn_setup():
        import jax, jax.numpy as jnp
        import numpy as np
        HEADS = 20
        NUM_TOKENS = 4
        IP_SCALE = 1.0
        SEM_SCALE = 0.5
        RESCALE = 1.0
        EPS = 1e-12

        def _l2norm(x, axis=-1):
            n = jnp.sqrt(jnp.sum(x * x, axis=axis, keepdims=True))
            return x / jnp.maximum(n, EPS)
        key = jax.random.key(seed)
        ks = jax.random.split(key, 10)
        B, S, C = (2, 256, 320)
        T, E = (81, 512)
        inp = {'hidden_states': jax.random.normal(ks[0], (B, S, C), jnp.float32), 'encoder_hidden_states': jax.random.normal(ks[1], (B, T, E), jnp.float32), 'spatial_mask': jax.random.uniform(ks[2], (S,), jnp.float32), 'W_q': jax.random.normal(ks[3], (C, C), jnp.float32) * C ** (-0.5), 'W_k': jax.random.normal(ks[4], (E, C), jnp.float32) * E ** (-0.5), 'W_v': jax.random.normal(ks[5], (E, C), jnp.float32) * E ** (-0.5), 'W_k_ip': jax.random.normal(ks[6], (E, C), jnp.float32) * E ** (-0.5), 'W_v_ip': jax.random.normal(ks[7], (E, C), jnp.float32) * E ** (-0.5), 'W_out': jax.random.normal(ks[8], (C, C), jnp.float32) * C ** (-0.5), 'b_out': jnp.zeros((C,), jnp.float32)}
        return inp
    _L1_xattn_all = _L1_xattn_setup()
    _L1_xattn_in = {k: v for k, v in _L1_xattn_all.items() if k in ('W_q', 'W_k', 'W_v', 'W_k_ip', 'W_v_ip', 'W_out', 'b_out')}
    del _L1_xattn_all
    return {'x': x, 'ctx_2048': ctx_2048, 'fside_S_0': fside_S_0, 'L0_xattn_Wq': _L0_xattn_in['Wq'], 'L0_xattn_Wk': _L0_xattn_in['Wk'], 'L0_xattn_Wv': _L0_xattn_in['Wv'], 'L0_xattn_Wk_ip': _L0_xattn_in['Wk_ip'], 'L0_xattn_Wv_ip': _L0_xattn_in['Wv_ip'], 'L0_xattn_Wo': _L0_xattn_in['Wo'], 'L0_xattn_bo': _L0_xattn_in['bo'], 'L1_xattn_W_q': _L1_xattn_in['W_q'], 'L1_xattn_W_k': _L1_xattn_in['W_k'], 'L1_xattn_W_v': _L1_xattn_in['W_v'], 'L1_xattn_W_k_ip': _L1_xattn_in['W_k_ip'], 'L1_xattn_W_v_ip': _L1_xattn_in['W_v_ip'], 'L1_xattn_W_out': _L1_xattn_in['W_out'], 'L1_xattn_b_out': _L1_xattn_in['b_out']}

def reference(x, ctx_2048, fside_S_0, L0_xattn_Wq, L0_xattn_Wk, L0_xattn_Wv, L0_xattn_Wk_ip, L0_xattn_Wv_ip, L0_xattn_Wo, L0_xattn_bo, L1_xattn_W_q, L1_xattn_W_k, L1_xattn_W_v, L1_xattn_W_k_ip, L1_xattn_W_v_ip, L1_xattn_W_out, L1_xattn_b_out):
    import jax
    import jax.numpy as jnp

    def _L0_xattn_ref(hidden_states, encoder_hidden_states, Wq, Wk, Wv, Wk_ip, Wv_ip, Wo, bo):
        import jax, jax.numpy as jnp
        import numpy as np
        NUM_HEADS = 20
        TEXT_LEN = 77
        IP_SCALE = 1.0

        def _attend(q, k, v, sm_scale):
            scores = jnp.einsum('bhsd,bhld->bhsl', q, k) * sm_scale
            probs = jax.nn.softmax(scores, axis=-1)
            return jnp.einsum('bhsl,bhld->bhsd', probs, v)

        def _split_heads(x, h):
            b, s, c = x.shape
            return x.reshape(b, s, h, c // h).transpose(0, 2, 1, 3)

        def _merge_heads(x):
            b, h, s, d = x.shape
            return x.transpose(0, 2, 1, 3).reshape(b, s, h * d)
        residual = hidden_states
        B, S, C = hidden_states.shape
        H = NUM_HEADS
        D = C // H
        sm_scale = 1.0 / jnp.sqrt(jnp.asarray(D, hidden_states.dtype))
        text = encoder_hidden_states[:, :TEXT_LEN, :]
        ip = encoder_hidden_states[:, TEXT_LEN:, :]
        q = _split_heads(hidden_states @ Wq.T, H)
        k = _split_heads(text @ Wk.T, H)
        v = _split_heads(text @ Wv.T, H)
        out_text = _merge_heads(_attend(q, k, v, sm_scale))
        k_ip = _split_heads(ip @ Wk_ip.T, H)
        v_ip = _split_heads(ip @ Wv_ip.T, H)
        out_ip = _merge_heads(_attend(q, k_ip, v_ip, sm_scale))
        out = out_text + IP_SCALE * out_ip
        out = out @ Wo.T + bo
        return out + residual

    def _L1_xattn_ref(hidden_states, encoder_hidden_states, spatial_mask, W_q, W_k, W_v, W_k_ip, W_v_ip, W_out, b_out):
        import jax, jax.numpy as jnp
        import numpy as np
        HEADS = 20
        NUM_TOKENS = 4
        IP_SCALE = 1.0
        SEM_SCALE = 0.5
        RESCALE = 1.0
        EPS = 1e-12

        def _l2norm(x, axis=-1):
            n = jnp.sqrt(jnp.sum(x * x, axis=axis, keepdims=True))
            return x / jnp.maximum(n, EPS)
        B, S, C = hidden_states.shape
        H = HEADS
        Dh = C // H
        attn_scale = Dh ** (-0.5)
        residual = hidden_states
        text_ehs = encoder_hidden_states[:, :-NUM_TOKENS]
        ip_ehs = encoder_hidden_states[:, -NUM_TOKENS:]

        def heads(x):
            return x.reshape(B, -1, H, Dh).transpose(0, 2, 1, 3)
        q = heads(hidden_states @ W_q)
        k_t = heads(text_ehs @ W_k)
        v_t = heads(text_ehs @ W_v)
        scores_t = jnp.einsum('bhsd,bhtd->bhst', q, k_t) * attn_scale
        probs_t = jax.nn.softmax(scores_t, axis=-1)
        text_out = jnp.einsum('bhst,bhtd->bhsd', probs_t, v_t)
        text_out = text_out.transpose(0, 2, 1, 3).reshape(B, S, C)
        k_ip = heads(ip_ehs @ W_k_ip)
        v_ip = heads(ip_ehs @ W_v_ip)
        attn_scores = jnp.einsum('bhsd,bhnd->bhsn', q, k_ip) * attn_scale
        qsem = jnp.einsum('bhst,bte->bhse', probs_t, text_ehs)
        qsem = _l2norm(qsem)
        ip_n = _l2norm(ip_ehs)
        sem = jnp.einsum('bhse,bne->bhsn', qsem, ip_n)
        sem = jax.lax.stop_gradient(sem)
        fused = attn_scores + SEM_SCALE * sem
        probs_ip = jax.nn.softmax(fused, axis=-1)
        probs_ip = probs_ip * spatial_mask[None, None, :, None]
        ip_out = jnp.einsum('bhsn,bhnd->bhsd', probs_ip, v_ip)
        ip_out = ip_out.transpose(0, 2, 1, 3).reshape(B, S, C)
        out = text_out + IP_SCALE * ip_out
        out = out @ W_out + b_out
        out = out + residual
        return out / RESCALE
    x = _L0_xattn_ref(x, ctx_2048, L0_xattn_Wq, L0_xattn_Wk, L0_xattn_Wv, L0_xattn_Wk_ip, L0_xattn_Wv_ip, L0_xattn_Wo, L0_xattn_bo)
    x = _L1_xattn_ref(x, ctx_2048, fside_S_0, L1_xattn_W_q, L1_xattn_W_k, L1_xattn_W_v, L1_xattn_W_k_ip, L1_xattn_W_v_ip, L1_xattn_W_out, L1_xattn_b_out)
    return x

_drawn_inputs = setup_inputs


def setup_inputs(seed=0):
    import zlib

    import numpy as np

    out = dict(_drawn_inputs(seed))
    spreads = {'L0_xattn_bo': (0.0, 0.1), 'L1_xattn_b_out': (0.0, 0.1)}
    factors = {}
    for name, (base, spread) in spreads.items():
        noise = np.random.default_rng([zlib.crc32(name.encode()), seed]).standard_normal(out[name].shape)
        drawn = base * np.exp(spread * noise) if base else spread * noise
        out[name] = jnp.asarray(drawn.astype(out[name].dtype))
    for name, factor in factors.items():
        out[name] = (out[name] * factor).astype(out[name].dtype)
    return out
```

```python
from contextlib import ExitStack

import numpy as np

import concourse.bass as bass
from concourse import mybir

F32 = mybir.dt.float32
F32R = mybir.dt.float32r
ALU = mybir.AluOpType
ACT = mybir.ActivationFunctionType
AX = mybir.AxisListType.X

B, S, C, E, H, D = 8, 256, 320, 512, 20, 16
TXT0 = 77
TXT1 = 252
NIP = 4
KC = 3
EC = 4
NG = 5
KT = S + 4
ROWS = 48
SROWS = 52
BASE = (0, 64)
PR = 8
CHUNK = (128, 128, 64)


def call(fn, *args, **kwargs):
    return fn, args, kwargs


class Queue:

    def __init__(self, engine, sem):
        self.engine, self.sem, self.n, self.ops, self.met = engine, sem, 0, [], {}

    def wait(self, *marks):
        for m in marks:
            if m is None:
                continue
            sem, value = m
            if self.met.get(id(sem), 0) < value:
                self.met[id(sem)] = value
                self.ops.append((call(self.engine.wait_ge, sem, value), None, 0))

    def do(self, what, sem=None):
        self.ops.append((what, sem, 16))

    def sig(self, what):
        self.n += 1
        self.ops.append((what, self.sem, 1))
        return (self.sem, self.n)

    def run(self, e):
        for (fn, args, kwargs), sem, by in self.ops:
            made = fn(*args, **kwargs)
            if sem is not None:
                made.then_inc(sem, by)


class Landing:

    def __init__(self, sem):
        self.sem, self.n = sem, 0

    def add(self):
        self.n += 16
        return self.sem

    def all(self):
        return (self.sem, self.n)


class Bank:
    def __init__(self, ap):
        self.ap, self.free = ap, []


def build(nc, xT, cT, cipT, fs, Wq0, Wk0, Wv0, Wki0, Wvi0, Wo0, bo0,
          Wq1, Wk1, Wv1, Wki1, Wvi1, Wo1, bo1, ident_d, ind_d, hm_d, outT):
    U = 2 * B
    with ExitStack() as ctx:
        def sb(name, shape, dt=F32):
            return ctx.enter_context(nc.sbuf_tensor(name, shape, dt))

        def ps(name):
            return ctx.enter_context(nc.psum_tensor(name, [128, 512], F32))

        def sem(name):
            return ctx.enter_context(nc.semaphore(name))

        PE = Queue(nc.tensor, sem("s_pe"))
        AC = Queue(nc.scalar, sem("s_act"))
        DV = Queue(nc.vector, sem("s_dve"))
        PO = Queue(nc.gpsimd, sem("s_pool"))
        SP = Queue(nc.sync, sem("s_sp"))

        x_sb = sb("x_sb", [128, KC, B * S])
        c_sb = [sb(f"c_sb{i}", [128, EC, S]) for i in range(2)]
        wq = [sb("wq", [128, KC, C])] * 2
        wo = [sb(f"wo{l}", [128, KC, C]) for l in range(2)]
        wki0 = sb("wki0", [128, EC, C])
        wvi0 = sb("wvi0", [128, EC, C])
        wk = [sb("wk0", [128, EC, C]), wki0]
        wv = [sb("wv0", [128, EC, C]), wvi0]
        bo = [sb(f"bo{l}", [128, KC]) for l in range(2)]
        ident = sb("ident", [128, 128])
        ones = sb("ones", [128, 128])
        mhalf = sb("mhalf", [128, 2 * H])
        fmask = sb("fmask", [128, 2])
        hmask = sb("hmask", [128, KC, H])
        ind_f = sb("ind_f", [4, 2, KT])
        ind = sb("ind", [4, 2, KT], F32R)
        big_f = sb("big_f", [H, S])
        big = sb("big", [H, S], F32R)
        QP = sb("QP", [128, H, S], F32R)
        KP = sb("KP", [128, H, KT], F32R)
        qhi = sb("qhi", [128, KC, S], F32R)
        qlo = sb("qlo", [128, KC, S], F32R)
        khi = sb("khi", [128, KC, KT], F32R)
        klo = sb("klo", [128, KC, KT], F32R)
        VX = [sb(f"VX{i}", [128, H, 32]) for i in range(3)]
        VY = [sb(f"VY{i}", [128, 2, H, 32]) for i in range(3)]
        P = sb("P", [128, PR, 2, S])
        Y = sb("Y", [128, PR, 2, S])
        y21 = sb("y21", [128, 32])
        GA = [v[:, :, :].rearrange("p h r -> p (h r)")[:, 0:128] for v in VX]
        GB = [v[:, :, :].rearrange("p h r -> p (h r)")[:, 128:384] for v in VX]
        Vs = [sb(f"Vs{i}", [128, 512]) for i in range(2)]
        O = [sb(f"O{i}", [128, 2, C]) for i in range(2)]
        rs = sb("rs", [128, 4, 4])
        ta = sb("ta", [128, 2, 64])
        tb = sb("tb", [128, 2, 64])
        aT = sb("aT", [128, KC, S])
        m_sb = sb("m_sb", [128, 2, 2 * H])
        mhi = sb("mhi", [2 * H, S], F32R)
        mlo = sb("mlo", [2 * H, S], F32R)
        ipS = [sb(f"ipS{i}", [128, 2, H, NIP]) for i in range(3)]
        ST = sb("ST", [128, 2, H, 6])
        cip = sb("cip", [128, EC, B * NIP])
        csq = sb("csq", [128, EC, B * NIP])
        kip = sb("kip", [128, KC, B * NIP])
        vip = sb("vip", [128, KC, B * NIP])
        invip = sb("invip", [128, B * NIP])
        nrm = sb("nrm", [128, B * NIP])
        bd = sb("bd", [128, KC, H, NIP])
        Mb = [sb("Mb", [H * NIP, C])] * 2
        e2 = sb("e2", [128, 2, H])
        n2 = sb("n2", [128, 2, H])
        rn = sb("rn", [128, 2, H])
        t1 = sb("t1", [128, 2, H, NIP])
        t2 = f1 = f2 = t1
        ex = sb("ex", [128, 2, H, NIP])
        mx = sb("mx", [128, 2, H])
        sm = sb("sm", [128, 2, H])
        ri = sb("ri", [128, 2, H])
        rm = sb("rm", [128, 2, H])
        w4 = sb("w4", [128, 2, H, NIP])
        wT = sb("wT", [H * NIP, S])

        wki1 = Y[:, 0:3, :, :].rearrange("p a c s -> p (a c s)")[:, 0:EC * C].rearrange("p (k n) -> p k n", k=EC)
        wvi1 = Y[:, 3:6, :, :].rearrange("p a c s -> p (a c s)")[:, 0:EC * C].rearrange("p (k n) -> p k n", k=EC)

        S1 = Bank(ps("pS1"))
        S2 = [Bank(ps(f"pS2{i}")) for i in range(2)]
        PV = Bank(ps("pPV"))
        GP = [Bank(ps(f"pGP{i}")) for i in range(2)]
        MI = [Bank(ps(f"pMI{i}")) for i in range(2)]
        step = [-1]
        turn = [0, 0]

        def misc(line):
            turn[line] += 1
            return GP[line] if step[0] < B - 1 and turn[line] % 2 else MI[line]

        qd = [nc.dram_tensor(f"qd{u}", (2, C, S), F32, kind="Internal").ap() for u in range(U)]
        kd = [nc.dram_tensor(f"kd{u}", (2, C, KT), F32, kind="Internal").ap() for u in range(U)]

        l_x = [Landing(sem(f"l_x{b}")) for b in range(B)]
        l_c = [Landing(sem(f"l_c{i}")) for i in range(2)]
        l_w = {n: Landing(sem(f"l_w_{n}")) for n in
               ("q0", "k0", "v0", "o0", "q1", "k1", "v1", "o1", "ip1", "const", "row", "ind0", "ind1", "ind8", "ind9")}
        l_st = {(a, i): Landing(sem(f"l_st{a}{i}")) for a in "qk" for i in range(2)}
        l_ld = [[Landing(sem(f"l_ld{i}{g}")) for g in range(NG)] for i in range(2)]
        l_m = [Landing(sem(f"l_m{i}")) for i in range(2)]
        l_out = Landing(sem("l_out"))

        def load(dst, src, landing):
            s = landing.add()
            SP.do(call(nc.sync.dma_start, dst, src), s)
            return landing.all()

        def load320(dst, src, landing, lo, n):
            load(dst[:, 0:2, lo:lo + n], src[0:256, lo:lo + n].rearrange("(c p) n -> p c n", p=128), landing)
            return load(dst[0:64, 2, lo:lo + n], src[256:320, lo:lo + n], landing)

        def load512(dst, src, landing):
            return load(dst, src.rearrange("(c p) n -> p c n", p=128), landing)

        c_ready, c_free = {}, {}

        def load_ctx(u):
            SP.wait(c_free.get(u - 2))
            c_ready[u] = load512(c_sb[u % 2][:, :, :], cT[:, (u % B) * S:(u % B) * S + S], l_c[u % 2])

        x_ready = {}
        w_ready = {}
        w_ready["q0"] = load320(wq[0], Wq0, l_w["q0"], 0, C)
        x_ready[0] = load320(x_sb, xT, l_x[0], 0, S)
        load_ctx(0)
        load512(wk[0][:, :, :], Wk0, l_w["k0"])
        w_ready["k0"] = load512(wki0[:, :, :], Wki0, l_w["k0"])
        load512(wv[0][:, :, :], Wv0, l_w["v0"])
        w_ready["v0"] = load512(wvi0[:, :, :], Wvi0, l_w["v0"])
        load(ident[:, :], ident_d, l_w["const"])
        load(ind_f[:, :, :], ind_d, l_w["const"])
        load(hmask[:, :, :], hm_d, l_w["const"])
        load(fmask[:, :], fs, l_w["const"])
        load(bo[0][:, :], bo0, l_w["const"])
        load(bo[1][:, :], bo1, l_w["const"])
        consts = load512(cip[:, :, :], cipT, l_w["const"])
        x_ready[1] = load320(x_sb, xT, l_x[1], S, S)
        load_ctx(1)
        w_ready["o0"] = load320(wo[0], Wo0, l_w["o0"], 0, C)
        for b in range(2, B):
            x_ready[b] = load320(x_sb, xT, l_x[b], b * S, S)
        load512(wki1, Wki1, l_w["ip1"])
        w_ready["ip1"] = load512(wvi1, Wvi1, l_w["ip1"])
        w_ready["o1"] = load320(wo[1], Wo1, l_w["o1"], 0, C)

        AC.wait(consts)
        ind_ready = AC.sig(call(nc.scalar.activation, ind[:, :, :], ind_f[:, :, :], ACT.Copy))
        big_f_set = DV.sig(call(nc.vector.memset, big_f[:, :], 30000.0))
        DV.sig(call(nc.vector.memset, ones[:, :], 1.0))
        mh_set = PO.sig(call(nc.gpsimd.memset, mhalf[:, :], -0.5))
        PO.wait(mh_set)
        DV.sig(call(nc.vector.memset, y21[:, :], 0.0))
        y21_zero = (DV.sem, DV.n)
        DV.wait(y21_zero)
        ones_set = DV.sig(call(nc.vector.memset, y21[:, 21:22], 1.0))
        for i in range(3):
            DV.sig(call(nc.vector.memset, VX[i][:, :, :], 0.0))
            z = DV.sig(call(nc.vector.memset, VY[i][:, :, :, :], 0.0))
            DV.wait(z)
            DV.sig(call(nc.vector.memset, VX[i][:, :, 16:17], 1.0))
            DV.sig(call(nc.vector.memset, VY[i][:, 1, :, 16:17], 1.0))
            z = DV.sig(call(nc.vector.memset, VY[i][64:128, 0, :, 16:17], 1.0))
            DV.wait(z)
            DV.sig(call(nc.vector.memset, VY[i][64:TXT0, 0, :, 16:17], 0.0))
        v_set = (DV.sem, DV.n)
        DV.sig(call(nc.vector.memset, khi[:, :, S:KT].bitcast(F32), 0.0))
        k_zero = DV.sig(call(nc.vector.memset, klo[:, :, S:KT].bitcast(F32), 0.0))
        AC.wait(big_f_set)
        big_ready = AC.sig(call(nc.scalar.activation, big[:, :], big_f[:, :], ACT.Copy))

        x1_ready = {}
        st_done = {}
        ld_done = {}
        s2_done = {}
        m_ready = {}
        v_ready = {}
        g_ready = {}
        mb_ready = {}
        kip_ready = [None]
        vip_ready = [None]
        invip_ready = [None]
        pv_done = {}
        gp_read = {}
        Vs_free = {}
        O_free = {}
        st = {"q_hi": None, "q_lo": None, "k_hi": None, "k_lo": None, "ST": None, "aT": None,
              "m": [], "mT": None, "wT": None, "bd": None, "ind": {}}

        def project(u, which, part):
            L, b = divmod(u, B)
            bank = misc(1)
            chunks = (0, 1) if part == 0 else (2,)
            hi, lo = (qhi, qlo) if which == "q" else (khi, klo)
            PE.wait(*bank.free)
            if which == "q":
                PE.wait(w_ready[f"q{L}"], x_ready[b] if L == 0 else x1_ready[b])
            else:
                PE.wait(w_ready[f"k{L}"], c_ready[u])
            c = c_sb[u % 2]
            for n, m in enumerate(chunks):
                M = CHUNK[m]
                if which == "q":
                    jobs = [(0, S, wq[L], x_sb, b * S, KC)]
                elif L == 0:
                    jobs = [(0, TXT0, wk[0], c, 0, EC), (TXT0, S, wki0, c, 0, EC)]
                else:
                    jobs = [(0, S, wk[1], c, 0, EC)]
                for t0, t1_, w, src, off, nk in jobs:
                    for k in range(nk):
                        K = CHUNK[k] if nk == KC else 128
                        fn = (call(nc.tensor.matmul, bank.ap[0:M, n * S + t0:n * S + t1_], w[0:K, k, m * 128:m * 128 + M],
                                       src[0:K, k, off + t0:off + t1_], start=(k == 0), stop=(k == nk - 1)))
                        if n == len(chunks) - 1 and t1_ == S and k == nk - 1:
                            done = PE.sig(fn)
                        else:
                            PE.do(fn)
            yield
            M = 128 if part == 0 else 64
            c0, c1 = chunks[0], chunks[-1] + 1
            src = bank.ap[0:M, 0:len(chunks) * S].rearrange("p (c s) -> p c s", s=S)
            d0, d1, s0, s1_ = 0, S, 0, S
            if which == "k" and L == 1:
                d0, d1, s0, s1_ = NIP, S, 0, TXT1
            AC.wait(done, st[which + "_hi"], st[which + "_lo"], k_zero)
            th = AC.sig(call(nc.scalar.activation, hi[0:M, c0:c1, d0:d1], src[:, :, s0:s1_], ACT.Copy))
            if d0:
                AC.wait(kip_ready[0])
                thi = AC.sig(call(nc.scalar.activation, hi[0:M, c0:c1, 0:NIP], kip[0:M, c0:c1, NIP * b:NIP * b + NIP], ACT.Copy))
            else:
                thi = th
            yield
            DV.wait(done, th, st[which + "_hi"], st[which + "_lo"])
            tl = DV.sig(call(nc.vector.tensor_tensor, lo[0:M, c0:c1, d0:d1], src[:, :, s0:s1_],
                                                  hi[0:M, c0:c1, d0:d1].bitcast(F32), ALU.subtract))
            bank.free = [th, tl]
            if d0:
                DV.wait(thi, kip_ready[0])
                tl = DV.sig(call(nc.vector.tensor_tensor, lo[0:M, c0:c1, 0:NIP], kip[0:M, c0:c1, NIP * b:NIP * b + NIP],
                                                      hi[0:M, c0:c1, 0:NIP].bitcast(F32), ALU.subtract))
            dram = (qd if which == "q" else kd)[u]
            W = S if which == "q" else KT
            land = l_st[(which, u % 2)]
            for z, (tile, tok) in enumerate(((hi, thi), (lo, tl))):
                if part == 0:
                    d_ap = dram[z, 0:256, :].rearrange("(c p) n -> p c n", p=128)
                else:
                    d_ap = dram[z, 256:320, :].rearrange("(c p) n -> p c n", p=64)
                s = land.add()
                SP.wait(tok, k_zero)
                SP.do(call(nc.sync.dma_start, d_ap, tile[0:M, c0:c1, 0:W].bitcast(F32)), s)
            if part == 1:
                st_done[(u, which)] = land.all()
                st[which + "_hi"] = st[which + "_lo"] = land.all()

        def load_pack(u, g):
            base, land = BASE[u % 2], l_ld[u % 2][g]
            SP.wait(st_done[(u, "q")], st_done[(u, "k")], s2_done.get((u - 2, g)))
            hs = slice(4 * g, 4 * g + 4)
            for z, row in ((0, 0), (0, 16), (1, 32)):
                src = qd[u][z, 64 * g:64 * g + 64, :].rearrange("(h d) s -> d h s", d=D)
                s = land.add()
                SP.do(call(nc.sync.dma_start, QP[base + row:base + row + D, hs, :].bitcast(F32), src), s)
            for z, row in ((0, 0), (1, 16), (0, 32)):
                src = kd[u][z, 64 * g:64 * g + 64, :].rearrange("(h d) s -> d h s", d=D)
                s = land.add()
                SP.do(call(nc.sync.dma_start, KP[base + row:base + row + D, hs, :].bitcast(F32), src), s)
            ld_done[(u, g)] = land.all()

        def load_ind(u):
            base, L = BASE[u % 2], u // B
            SP.wait(ind_ready, s2_done.get((u - 2, NG - 1)))
            for h in range(0, H, 4):
                s = l_w[f"ind{u}"].add()
                SP.do(call(nc.sync.dma_start, KP[base + ROWS:base + SROWS, h:h + 4, :].bitcast(F32),
                                                      ind[:, L, None, :].to_broadcast([4, 4, KT]).bitcast(F32)), s)
            st["ind"][u] = l_w[f"ind{u}"].all()
            if L == 1:
                SP.wait(big_ready)
                for r in (50, 51):
                    s = l_w[f"ind{u}"].add()
                    SP.do(call(nc.sync.dma_start, QP[base + r:base + r + 1, :, :].bitcast(F32), big[:, :].bitcast(F32)), s)
                st["ind"][u] = l_w[f"ind{u}"].all()

        def values(u):
            L, b = divmod(u, B)
            c = c_sb[u % 2]
            tiles = ([(VX, None, 0, TXT0, wv[0]), (VY, 0, 0, 128, wvi0), (VY, 1, 128, 256, wvi0)] if L == 0 else
                     [(VY, 0, 0, 128, wv[1]), (VY, 1, 128, 256, wv[1])])
            old = [pv_done.get((u - 3, NG - 1))]
            for V, ch, t0, t1_, w in tiles:
                bank = misc(1)
                M = t1_ - t0
                PE.wait(*bank.free)
                PE.wait(w_ready[f"v{L}"], c_ready[u])
                for k in range(EC):
                    fn = (call(nc.tensor.matmul, bank.ap[0:M, 0:C], c[:, k, t0:t1_], w[:, k, :],
                                                  start=(k == 0), stop=(k == EC - 1)))
                    done = PE.sig(fn) if k == EC - 1 else PE.do(fn)
                c_free[u] = done
                yield
                src = bank.ap[:, 0:C].rearrange("p (h d) -> p h d", d=D)
                AC.wait(done, v_set, *old)
                if L == 0 and ch is None:
                    v_ready[u] = [AC.sig(call(nc.scalar.activation, V[u % 3][0:M, :, 0:D], src[0:M], ACT.Copy))]
                    bank.free = [v_ready[u][0]]
                elif L == 0 and ch == 0:
                    t = AC.sig(call(nc.scalar.activation, V[u % 3][64:128, 0, :, 0:D], src[64:128], ACT.Copy))
                    bank.free = [t]
                    DV.wait(t)
                    t = DV.sig(call(nc.vector.memset, V[u % 3][64:TXT0, 0, :, 0:D], 0.0))
                    v_ready[u].append(t)
                else:
                    t = AC.sig(call(nc.scalar.activation, V[u % 3][:, ch, :, 0:D], src, ACT.Copy))
                    bank.free = [t]
                    v_ready.setdefault(u, []).append(t)
                yield

        def gram(u):
            c = c_sb[u % 2]
            i = u % 3
            for ch in range(2):
                bank = misc(1)
                PE.wait(*bank.free)
                PE.wait(c_ready[u])
                for k in range(EC):
                    fn = (call(nc.tensor.matmul, bank.ap[:, 0:S], c[:, k, 128 * ch:128 * ch + 128], c[:, k, :],
                                                  start=(k == 0), stop=(k == EC - 1)))
                    done = PE.sig(fn) if k == EC - 1 else PE.do(fn)
                c_free[u] = done
                yield
                AC.wait(done, gp_read.get(u - 3), pv_done.get((u - 3, NG - 1)))
                if ch == 0:
                    ta_ = AC.sig(call(nc.scalar.activation, GA[i][:, :], bank.ap[:, 0:128], ACT.Copy))
                    toks = [ta_]
                else:
                    AC.sig(call(nc.scalar.activation, GB[i][:, 0:128], bank.ap[:, 0:128], ACT.Copy, scale=2.0))
                    ta_ = AC.sig(call(nc.scalar.activation, GB[i][:, 128:256], bank.ap[:, 128:256], ACT.Copy))
                    toks = [ta_]
                DV.wait(toks[-1], v_set, pv_done.get((u - 3, NG - 1)))
                z = DV.sig(call(nc.vector.tensor_copy, VY[i][:, ch, :, 16:20],
                                                          bank.ap[:, None, TXT1:S].to_broadcast([128, H, NIP])))
                if u < B + 3:
                    DV.wait(z)
                    z = DV.sig(call(nc.vector.memset, VY[i][:, ch, :, 20:21], 1.0))
                bank.free = toks + [z]
                g_ready.setdefault(u, []).extend(toks)
                v_ready.setdefault(u, []).append(z)
                yield

        def ip_prep():
            for w, dst, hold in ((wki1, kip, kip_ready), (wvi1, vip, vip_ready)):
                bank = misc(1)
                PE.wait(*bank.free)
                PE.wait(w_ready["ip1"], consts)
                for m in range(KC):
                    M = CHUNK[m]
                    for k in range(EC):
                        fn = (call(nc.tensor.matmul, 
                            bank.ap[0:M, 32 * m:32 * m + 32], w[:, k, m * 128:m * 128 + M], cip[:, k, :],
                            start=(k == 0), stop=(k == EC - 1)))
                        done = PE.sig(fn) if (m == 2 and k == EC - 1) else PE.do(fn)
                yield
                AC.wait(done)
                AC.sig(call(nc.scalar.activation, 
                    dst[:, 0:2, :], bank.ap[:, 0:64].rearrange("p (c n) -> p c n", n=32), ACT.Copy))
                hold[0] = AC.sig(call(nc.scalar.activation, dst[0:64, 2, :], bank.ap[0:64, 64:96], ACT.Copy))
                bank.free = [hold[0]]
                yield
            DV.wait(consts)
            sq = DV.sig(call(nc.vector.tensor_tensor, csq[:, :, :], cip[:, :, :], cip[:, :, :], ALU.mult))
            yield
            bank = misc(1)
            PE.wait(*bank.free)
            PE.wait(sq, ones_set)
            for k in range(EC):
                fn = (call(nc.tensor.matmul, bank.ap[:, 0:32], ones[:, :], csq[:, k, :],
                                              start=(k == 0), stop=(k == EC - 1)))
                done = PE.sig(fn) if k == EC - 1 else PE.do(fn)
            yield
            DV.wait(done)
            z = DV.sig(call(nc.vector.tensor_scalar, nrm[:, :], bank.ap[:, 0:32], 1e-24, None, ALU.max))
            bank.free = [z]
            PO.wait(z)
            invip_ready[0] = PO.sig(call(nc.gpsimd.tensor_tensor, invip[:, :], nrm[:, :], mhalf[:, 0:B * NIP], ALU.pow))
            yield

        def ip_values(u):
            b = u % B
            DV.wait(vip_ready[0], consts, st["bd"])
            src = vip[:, 0:2, None, NIP * b:NIP * b + NIP].to_broadcast([128, 2, H, NIP])
            DV.sig(call(nc.vector.tensor_tensor, bd[:, 0:2, :, :], src,
                                             hmask[:, 0:2, :, None].to_broadcast([128, 2, H, NIP]), ALU.mult))
            t = DV.sig(call(nc.vector.tensor_tensor, bd[0:64, 2, :, :],
                                                 vip[0:64, 2, None, NIP * b:NIP * b + NIP].to_broadcast([64, H, NIP]),
                                                 hmask[0:64, 2, :, None].to_broadcast([64, H, NIP]), ALU.mult))
            yield
            bank = misc(0)
            PE.wait(*bank.free)
            PE.wait(t, w_ready["o1"])
            for k in range(KC):
                K = CHUNK[k]
                fn = (call(nc.tensor.matmul, bank.ap[0:H * NIP, 0:C],
                                                   bd[0:K, k, :, :].rearrange("p h n -> p (h n)"), wo[1][0:K, k, :],
                                                   start=(k == 0), stop=(k == KC - 1)))
                done = PE.sig(fn) if k == KC - 1 else PE.do(fn)
            st["bd"] = done
            yield
            AC.wait(done, x1_ready.get(("out", u - 1)))
            mb_ready[u] = AC.sig(call(nc.scalar.activation, Mb[u % 2][:, :], bank.ap[0:H * NIP, 0:C], ACT.Copy))
            bank.free = [mb_ready[u]]
            yield

        def prepare(u):
            L = u // B
            yield from project(u, "q", 0)
            yield
            yield from project(u, "q", 1)
            yield
            yield from project(u, "k", 0)
            yield
            yield from project(u, "k", 1)
            yield
            yield from values(u)
            if L == 1:
                yield from gram(u)

        ip_copied = {}

        def score_max(u, h):
            L, base = u // B, BASE[u % 2]
            PE.wait(ld_done[(u, h // 4)], *S1.free)
            for sc in range(2):
                fn = (call(nc.tensor.matmul, S1.ap[:, sc * S:sc * S + S],
                                                QP[base:base + ROWS, h, sc * 128:sc * 128 + 128],
                                                KP[base:base + ROWS, h, 0:S], start=True, stop=True))
                done = PE.sig(fn) if sc else PE.do(fn)
            v = S1.ap[:, :].rearrange("p (c t) -> p c t", c=2)
            DV.wait(done, *st["m"])
            if L == 0:
                DV.sig(call(nc.vector.tensor_reduce, m_sb[:, :, h], v[:, :, 0:TXT0], AX, ALU.max))
                t = DV.sig(call(nc.vector.tensor_reduce, m_sb[:, :, H + h], v[:, :, TXT0:S], AX, ALU.max))
                S1.free = [t]
            else:
                t = DV.sig(call(nc.vector.tensor_reduce, m_sb[:, :, h], v[:, :, NIP:S], AX, ALU.max))
                DV.wait(x1_ready.get(("ip", u - 3)))
                t2_ = DV.sig(call(nc.vector.tensor_copy, ipS[u % 3][:, :, h, :], v[:, :, 0:NIP]))
                S1.free = [t, t2_]
                ip_copied[u] = t2_
            m_ready[u] = t

        def shift_rows(u):
            L, base = u // B, BASE[u % 2]
            R = 2 * H if L == 0 else H
            bank = misc(0)
            PE.wait(*bank.free)
            PE.wait(m_ready[u], consts)
            for sc in range(2):
                fn = (call(nc.tensor.transpose, bank.ap[0:R, sc * 128:sc * 128 + 128], m_sb[:, sc, 0:R], ident[:, :]))
                done = PE.sig(fn) if sc else PE.do(fn)
            st["m"] = [done]
            AC.wait(done, st["mT"])
            th = AC.sig(call(nc.scalar.activation, mhi[0:R, :], bank.ap[0:R, 0:S], ACT.Copy))
            DV.wait(done, th, st["mT"])
            tl = DV.sig(call(nc.vector.tensor_tensor, mlo[0:R, :], bank.ap[0:R, 0:S], mhi[0:R, :].bitcast(F32), ALU.subtract))
            bank.free = [th, tl]
            SP.wait(th, s2_done.get((u - 2, NG - 1)))
            rows = [(48, mhi, 0), (50, mhi, H), (49, mlo, 0), (51, mlo, H)] if L == 0 else [(48, mhi, 0), (49, mlo, 0)]
            for r, tile, h0 in rows:
                if tile is mlo:
                    SP.wait(tl)
                s = l_m[u % 2].add()
                SP.do(call(nc.sync.dma_start, 
                    QP[base + r:base + r + 1, :, :].bitcast(F32), tile[h0:h0 + H, :].bitcast(F32)), s)
            m_ready[u] = st["mT"] = l_m[u % 2].all()

        exp_done = {}
        y_done = {}

        def scores(u, h):
            L, base = u // B, BASE[u % 2]
            off = NIP if L else 0
            n = u * H + h
            bank = S2[n % 2]
            PE.wait(m_ready[u], ld_done[(u, h // 4)], st["ind"][u if u < 2 else (B + u % 2 if L else u % 2)], *bank.free)
            for ch in range(2):
                fn = (call(nc.tensor.matmul, bank.ap[:, ch * S:ch * S + S],
                                                KP[base:base + SROWS, h, off + ch * 128:off + ch * 128 + 128],
                                                QP[base:base + SROWS, h, :], start=True, stop=True))
                done = PE.sig(fn) if ch else PE.do(fn)
            if h % 4 == 3:
                s2_done[(u, h // 4)] = done
            p = n % PR
            AC.wait(done, pv_done.get(divmod(n - PR, H) if False else ((n - PR) // H, ((n - PR) % H) // 4)), y_done.get(n - PR))
            exp_done[n] = AC.sig(call(nc.scalar.activation, P[:, p, :, :], bank.ap[:, :].rearrange("p (c s) -> p c s", c=2),
                                                        ACT.Exp, scale=0.25))
            bank.free = [exp_done[n]]

        def quad(u, h):
            n, i = u * H + h, u % 3
            p = n % PR
            bank = GP[n % 2]
            PE.wait(exp_done[n], *g_ready[u])
            PE.wait(*bank.free)
            PE.do(call(nc.tensor.matmul, bank.ap[:, 0:S], GA[i][:, :], P[:, p, 0, :], start=True, stop=False))
            PE.do(call(nc.tensor.matmul, bank.ap[:, 0:S], GB[i][:, 0:128], P[:, p, 1, :], start=False, stop=True))
            done = PE.sig(call(nc.tensor.matmul, bank.ap[:, S:2 * S], GB[i][:, 128:256], P[:, p, 1, :], start=True, stop=True))
            gp_read[u] = done
            DV.wait(done, exp_done[n], pv_done.get(((n - PR) // H, ((n - PR) % H) // 4)), kip_ready[0], vip_ready[0])
            y_done[n] = DV.sig(call(nc.vector.tensor_tensor, Y[:, p, :, :], bank.ap[:, :].rearrange("p (c s) -> p c s", c=2),
                                                         P[:, p, :, :], ALU.mult))
            bank.free = [y_done[n]]

        vs_done = {}

        def weigh(u, g):
            L, i = u // B, u % 3
            last = u * H + 4 * g + 3
            PE.wait(exp_done[last], *v_ready[u])
            PE.wait(*PV.free)
            hs = [(j, 4 * g + j, (u * H + 4 * g + j) % PR) for j in range(4)]
            if L == 0:
                for j, h, p in hs:
                    PE.do(call(nc.tensor.matmul, PV.ap[32 * j:32 * j + 32, 0:S], VX[i][0:TXT0, h, :],
                                                            P[0:TXT0, p, 0, :], start=True, stop=True, tile_position=(0, 32 * j)))
                for ch in range(2):
                    for j, h, p in hs:
                        fn = (call(nc.tensor.matmul, 
                            PV.ap[32 * j:32 * j + 32, S:2 * S], VY[i][:, ch, h, :], P[:, p, ch, :],
                            start=(ch == 0), stop=(ch == 1), tile_position=(0, 32 * j)))
                        done = PE.sig(fn) if ch and j == 3 else PE.do(fn)
            else:
                PE.wait(ones_set)
                for ch in range(2):
                    for j, h, p in hs:
                        PE.do(call(nc.tensor.matmul, 
                            PV.ap[32 * j:32 * j + 32, 0:S], VY[i][:, ch, h, :], P[:, p, ch, :],
                            start=(ch == 0), stop=False, tile_position=(0, 32 * j)))
                PE.wait(y_done[last])
                for ch in range(2):
                    for j, h, p in hs:
                        fn = (call(nc.tensor.matmul, 
                            PV.ap[32 * j:32 * j + 32, 0:S], y21[:, :], Y[:, p, ch, :],
                            start=False, stop=(ch == 1), tile_position=(0, 32 * j)))
                        done = PE.sig(fn) if ch and j == 3 else PE.do(fn)
            pv_done[(u, g)] = done
            N = 2 * S if L == 0 else S
            k = (u * NG + g) % 2
            AC.wait(done, Vs_free.get(k))
            vs_done[(u, g)] = AC.sig(call(nc.scalar.activation, Vs[k][:, 0:N], PV.ap[:, 0:N], ACT.Copy))
            PV.free = [vs_done[(u, g)]]

        o_done = {}

        def normalize(u, g):
            L, k, i = u // B, (u * NG + g) % 2, u % 2
            nt = 4 if L == 0 else 2
            bank = misc(0)
            PE.wait(*bank.free)
            PE.wait(vs_done[(u, g)], consts)
            for t in range(nt):
                fn = (call(nc.tensor.transpose, bank.ap[:, 128 * t:128 * t + 128], Vs[k][:, 128 * t:128 * t + 128], ident[:, :]))
                done = PE.sig(fn) if t == nt - 1 else PE.do(fn)
            Vs_free[k] = done
            yield
            v = bank.ap[:, 0:128 * nt].rearrange("p (t j r) -> p t j r", t=nt, j=4)
            od = O[i][:, :, 64 * g:64 * g + 64]
            od4 = od.rearrange("p c (j d) -> p c j d", j=4)
            col = 16 if L == 0 else 20
            DV.wait(done, O_free.get(i), st.get("rs"))
            tr = DV.sig(call(nc.vector.reciprocal, rs[:, 0:nt, :], v[:, :, :, col]))
            DV.wait(tr)
            if L == 0:
                rb = rs[:, :, :, None].to_broadcast([128, 4, 4, D])
                t_a = DV.sig(call(nc.vector.tensor_tensor, ta[:, :, :].rearrange("p c (j d) -> p c j d", j=4), v[:, 0:2, :, 0:D], rb[:, 0:2], ALU.mult))
                t_b = DV.sig(call(nc.vector.tensor_tensor, tb[:, :, :].rearrange("p c (j d) -> p c j d", j=4), v[:, 2:4, :, 0:D], rb[:, 2:4], ALU.mult))
                bank.free = [t_b]
                DV.wait(t_b)
                st["rs"] = o_done[u] = DV.sig(call(nc.vector.tensor_tensor, od, ta[:, :, :], tb[:, :, :], ALU.add))
            else:
                rb = rs[:, 0:2, :, None].to_broadcast([128, 2, 4, D])
                st["rs"] = o_done[u] = DV.sig(call(nc.vector.tensor_tensor, od4, v[:, :, :, 0:D], rb, ALU.mult))
                DV.wait(st["ST"])
                t = DV.sig(call(nc.vector.tensor_copy, ST[:, :, 4 * g:4 * g + 4, :], v[:, :, :, 16:22]))
                bank.free = [t]
                st_done[("ST", u)] = t
            yield

        def finish(u):
            L, b = divmod(u, B)
            i = u % 2
            if L == 1:
                yield from ip_values(u)

                def dv(fn, *w):
                    DV.wait(*w)
                    return DV.sig(fn)
                bc = lambda a: a[:, :, :, None].to_broadcast([128, 2, H, NIP])
                t = dv(call(nc.vector.scalar_tensor_tensor, e2[:, :, :], ST[:, :, :, 4], 1e-24, ST[:, :, :, 4], ALU.mult, ALU.mult), st_done[("ST", u)])
                t = dv(call(nc.vector.tensor_tensor, n2[:, :, :], ST[:, :, :, 5], e2[:, :, :], ALU.max), t)
                PO.wait(t)
                t = PO.sig(call(nc.gpsimd.tensor_tensor, rn[:, :, :].rearrange("p c h -> p (c h)"), n2[:, :, :].rearrange("p c h -> p (c h)"), mhalf[:, :], ALU.pow))
                t = dv(call(nc.vector.tensor_tensor, t1[:, :, :, :], ST[:, :, :, 0:NIP], bc(rn), ALU.mult), t)
                st["ST"] = t
                iv = invip[:, None, NIP * b:NIP * b + NIP].to_broadcast([128, 2 * H, NIP])
                t = dv(call(nc.vector.tensor_tensor, t2[:, :, :, :].rearrange("p c h n -> p (c h) n"),
                                                 t1[:, :, :, :].rearrange("p c h n -> p (c h) n"), iv, ALU.mult), t, invip_ready[0])
                yield
                t = dv(call(nc.vector.scalar_tensor_tensor, f1[:, :, :, :], t2[:, :, :, :], 2.0, ipS[u % 3][:, :, :, :], ALU.mult, ALU.add), t, ip_copied[u])
                x1_ready[("ip", u)] = t
                t = dv(call(nc.vector.tensor_reduce, mx[:, :, :], f1[:, :, :, :], AX, ALU.max), t)
                t = dv(call(nc.vector.tensor_tensor, f2[:, :, :, :], f1[:, :, :, :], bc(mx), ALU.subtract), t)
                AC.wait(t)
                ta_ = AC.sig(call(nc.scalar.activation, ex[:, :, :, :], f2[:, :, :, :], ACT.Exp, scale=0.25))
                yield
                t = dv(call(nc.vector.tensor_reduce, sm[:, :, :], ex[:, :, :, :], AX, ALU.add), ta_)
                t = dv(call(nc.vector.reciprocal, ri[:, :, :], sm[:, :, :]), t)
                t = dv(call(nc.vector.tensor_tensor, rm[:, :, :], ri[:, :, :], fmask[:, :, None].to_broadcast([128, 2, H]), ALU.mult), t, consts)
                tw = dv(call(nc.vector.tensor_tensor, w4[:, :, :, :], ex[:, :, :, :], bc(rm), ALU.mult), t)
                yield
            bank = misc(0)
            bank2 = misc(0)
            PE.wait(*bank.free)
            PE.wait(o_done[u], consts)
            for k in range(2):
                for sc in range(2):
                    fn = (call(nc.tensor.transpose, bank.ap[:, k * S + sc * 128:k * S + sc * 128 + 128],
                                                            O[i][:, sc, 128 * k:128 * k + 128], ident[:, :]))
                    done = PE.sig(fn) if k and sc else PE.do(fn)
            AC.wait(done, st["aT"])
            tA = AC.sig(call(nc.scalar.activation, aT[:, 0:2, :], bank.ap[:, :].rearrange("p (c s) -> p c s", c=2), ACT.Copy))
            bank.free = [tA]
            yield
            PE.wait(*bank2.free)
            for sc in range(2):
                fn = (call(nc.tensor.transpose, bank2.ap[0:64, sc * 128:sc * 128 + 128], O[i][:, sc, 256:320], ident[:, :]))
                done2 = PE.sig(fn) if sc else PE.do(fn)
            O_free[i] = done2
            AC.wait(done2, st["aT"])
            tB = AC.sig(call(nc.scalar.activation, aT[0:64, 2, :], bank2.ap[0:64, 0:S], ACT.Copy))
            bank2.free = [tB]
            yield
            if L == 1:
                bank3 = misc(0)
                PE.wait(*bank3.free)
                PE.wait(tw)
                for sc in range(2):
                    fn = (call(nc.tensor.transpose, bank3.ap[0:H * NIP, sc * 128:sc * 128 + 128],
                                                       w4[:, sc, :, :].rearrange("p h n -> p (h n)"), ident[:, :]))
                    done = PE.sig(fn) if sc else PE.do(fn)
                AC.wait(done, st["wT"])
                tW = AC.sig(call(nc.scalar.activation, wT[:, :], bank3.ap[0:H * NIP, 0:S], ACT.Copy))
                bank3.free = [tW]
                yield
            for chunks in ((0, 1), (2,)):
                bank = misc(0)
                PE.wait(*bank.free)
                PE.wait(tA, tB, w_ready[f"o{L}"])
                if L == 1:
                    PE.wait(tW, mb_ready[u])
                for n, m in enumerate(chunks):
                    M = CHUNK[m]
                    for k in range(KC):
                        K = CHUNK[k]
                        final = k == KC - 1 and L == 0
                        fn = (call(nc.tensor.matmul, 
                            bank.ap[0:M, n * S:n * S + S], wo[L][0:K, k, m * 128:m * 128 + M], aT[0:K, k, :],
                            start=(k == 0), stop=final))
                        if final and m == chunks[-1]:
                            done = PE.sig(fn)
                        else:
                            PE.do(fn)
                    if L == 1:
                        fn = (call(nc.tensor.matmul, 
                            bank.ap[0:M, n * S:n * S + S], Mb[i][:, m * 128:m * 128 + M], wT[:, :], start=False, stop=True))
                        done = PE.sig(fn) if m == chunks[-1] else PE.do(fn)
                yield
                for n, m in enumerate(chunks):
                    M = CHUNK[m]
                    dst = x_sb[0:M, m, b * S:b * S + S]
                    DV.wait(done, x_ready[b], consts)
                    if L == 1:
                        DV.wait(x1_ready[b])
                    t = DV.sig(call(nc.vector.scalar_tensor_tensor, 
                        dst, bank.ap[0:M, n * S:n * S + S], bo[L][0:M, m:m + 1], dst, ALU.add, ALU.add))
                bank.free = [t]
                if L == 1:
                    SP.wait(t)
                    for m in chunks:
                        s = l_out.add()
                        SP.do(call(nc.sync.dma_start, 
                            outT[128 * m:128 * m + CHUNK[m], b * S:b * S + S],
                            x_sb[0:CHUNK[m], m, b * S:b * S + S]), s)
                yield
            st["aT"] = st["wT"] = done
            if L == 0:
                x1_ready[b] = t
            else:
                x1_ready[("out", u)] = done

        def drain(gens):
            for g in gens:
                for _ in g:
                    pass

        ahead, behind = [], []

        def advance(line, k):
            while k and line:
                try:
                    next(line[0][1])
                    k -= 1
                except StopIteration:
                    line.pop(0)

        def complete(key):
            while any(k == key for k, _ in behind):
                advance(behind, 1)

        drain([prepare(0)])
        load_ind(0)
        for g in range(NG):
            load_pack(0, g)
        load_ctx(2)
        drain([prepare(1)])
        load_ind(1)
        for g in range(NG):
            load_pack(1, g)
        for h in range(H):
            score_max(0, h)
        shift_rows(0)
        scores(0, 0)
        for u in range(U):
            step[0] = u
            if u + 3 < U:
                load_ctx(u + 3)
            if u + 2 < U:
                ahead.append((u + 2, prepare(u + 2)))
            if u == 2:
                ahead.append(("ip", ip_prep()))
            nxt = loads = 0
            for h in range(H):
                if h + 1 < H:
                    scores(u, h + 1)
                while u + 1 < U and nxt < min(H, (5 * (h + 1) + 3) // 4):
                    score_max(u + 1, nxt)
                    nxt += 1
                if u >= B:
                    quad(u, h)
                advance(behind, 2)
                advance(ahead, 2)
                if h % 4 == 1 and h > 4:
                    g = h // 4 - 1
                    complete((u, g - 2) if g > 1 else (u - 1, g + NG - 2))
                    weigh(u, g)
                    behind.append(((u, g), normalize(u, g)))
                while u + 2 < U and (u + 2, "k") in st_done and loads < NG and (u, loads) in s2_done:
                    load_pack(u + 2, loads)
                    loads += 1
                if h == 16 and u + 1 < U:
                    advance(behind, 1000)
                    shift_rows(u + 1)
            complete((u, NG - 3))
            weigh(u, NG - 1)
            behind.append(((u, NG - 1), normalize(u, NG - 1)))
            behind.append((("end", u), finish(u)))
            if u + 1 < U:
                scores(u + 1, 0)
            if u + 2 < U:
                advance(ahead, 1000)
                while loads < NG:
                    load_pack(u + 2, loads)
                    loads += 1
                if u + 2 in (B, B + 1):
                    load_ind(u + 2)
            if u == B - 3:
                SP.wait(c_free[B - 1])
                w_ready["q1"] = load320(wq[1], Wq1, l_w["q1"], 0, C)
                w_ready["k1"] = load512(wk[1][:, :, :], Wk1, l_w["k1"])
                w_ready["v1"] = load512(wv[1][:, :, :], Wv1, l_w["v1"])
        advance(behind, 10000)
        SP.wait(l_out.all())
        for land in list(l_w.values()) + l_x + l_c:
            SP.wait(land.all())

        block = ctx.enter_context(nc.Block())
        block.tensor(PE.run)
        block.scalar(AC.run)
        block.vector(DV.run)
        block.sync(SP.run)
        block.gpsimd(PO.run)


def kernel(**inputs):
    import numpy as _np
    import concourse.bacc as _bacc
    from concourse import mybir as _mybir
    from concourse.bass_utils import run_bass_kernel_spmd as _run

    g = {k: _np.asarray(v) for k, v in inputs.items()}
    T = lambda a: _np.ascontiguousarray(a.T)

    def col(v):
        out = _np.zeros((3, 128), v.dtype)
        out[0], out[1], out[2, :64] = v[0:128], v[128:256], v[256:320]
        return T(out)

    ctx = g["ctx_2048"]
    ind = _np.zeros((4, 2, KT), _np.float32)
    ind[0:2, 0, 0:TXT0] = -1.0
    ind[2:4, 0, TXT0:S] = -1.0
    ind[0:2, 1, NIP:S] = -1.0
    ind[2, 1, S:KT] = -1.0
    hm = _np.zeros((128, 3, H), _np.float32)
    for c in range(C):
        hm[c % 128, c // 128, c // D] = 1.0
    arrays = {
        "xT": T(g["x"].reshape(B * S, C)),
        "cT": T(ctx.reshape(B * S, E)),
        "cipT": T(ctx[:, TXT1:, :].reshape(B * NIP, E)),
        "fs": T(g["fside_S_0"].reshape(2, 128)),
        "Wq0": T(g["L0_xattn_Wq"]), "Wk0": T(g["L0_xattn_Wk"]), "Wv0": T(g["L0_xattn_Wv"]),
        "Wki0": T(g["L0_xattn_Wk_ip"]), "Wvi0": T(g["L0_xattn_Wv_ip"]), "Wo0": T(g["L0_xattn_Wo"]),
        "bo0": col(g["L0_xattn_bo"]),
        "Wq1": g["L1_xattn_W_q"], "Wk1": g["L1_xattn_W_k"], "Wv1": g["L1_xattn_W_v"],
        "Wki1": g["L1_xattn_W_k_ip"], "Wvi1": g["L1_xattn_W_v_ip"], "Wo1": g["L1_xattn_W_out"],
        "bo1": col(g["L1_xattn_b_out"]),
        "ident": _np.eye(128, dtype=_np.float32), "ind": ind, "hm": hm,
    }
    nc = _bacc.Bacc("TRN2", target_bir_lowering=False, num_devices=1)
    args, feeds = [], {}
    for name, a in arrays.items():
        a = _np.ascontiguousarray(a)
        feeds[f"in_{name}"] = a
        args.append(nc.dram_tensor(f"in_{name}", a.shape, _mybir.dt.from_np(a.dtype), kind="ExternalInput").ap())
    args.append(nc.dram_tensor("out_T", (C, B * S), _mybir.dt.float32, kind="ExternalOutput").ap())
    build(nc, *args)
    r = _run(nc, [feeds], core_ids=[0])
    got = r.results[0]["out_T"]
    return _np.ascontiguousarray(got.T).reshape(B, S, C)
```

```python
from contextlib import ExitStack

import numpy as np

import concourse.bass as bass
from concourse import mybir

F32 = mybir.dt.float32
F32R = mybir.dt.float32r
ALU = mybir.AluOpType
ACT = mybir.ActivationFunctionType
AX = mybir.AxisListType.X

B, S, C, E, H, D = 8, 256, 320, 512, 20, 16
TXT0 = 77
TXT1 = 252
NIP = 4
KC = 3
EC = 4
NG = 5
KT = S + 4
ROWS = 48
SROWS = 52
BASE = (0, 64)
PR = 6
MH = 14
HR = 3
VS = 22
VW = H * VS + 10
CHUNK = (128, 128, 64)


def call(fn, *args, **kwargs):
    return fn, args, kwargs


class Queue:

    def __init__(self, engine, sem):
        self.engine, self.sem, self.n, self.ops, self.met = engine, sem, 0, [], {}

    def wait(self, *marks):
        for m in marks:
            if m is None:
                continue
            sem, value = m
            if self.met.get(id(sem), 0) < value:
                self.met[id(sem)] = value
                self.ops.append((call(self.engine.wait_ge, sem, value), None, 0))

    def do(self, what, sem=None):
        self.ops.append((what, sem, 16))

    def sig(self, what):
        self.n += 1
        self.ops.append((what, self.sem, 1))
        return (self.sem, self.n)

    def run(self, e):
        for (fn, args, kwargs), sem, by in self.ops:
            made = fn(*args, **kwargs)
            if sem is not None:
                made.then_inc(sem, by)


class Landing:

    def __init__(self, sem):
        self.sem, self.n = sem, 0

    def add(self):
        self.n += 16
        return self.sem

    def all(self):
        return (self.sem, self.n)


class Bank:
    def __init__(self, ap):
        self.ap, self.free = ap, []


def build(nc, xT, cT, cipT, fs, Wq0, Wk0, Wv0, Wki0, Wvi0, Wo0, bo0,
          Wq1, Wk1, Wv1, Wki1, Wvi1, Wo1, bo1, ident_d, ind_d, hm_d, outT):
    U = 2 * B
    with ExitStack() as ctx:
        def sb(name, shape, dt=F32):
            return ctx.enter_context(nc.sbuf_tensor(name, shape, dt))

        def ps(name):
            return ctx.enter_context(nc.psum_tensor(name, [128, 512], F32))

        def sem(name):
            return ctx.enter_context(nc.semaphore(name))

        PE = Queue(nc.tensor, sem("s_pe"))
        AC = Queue(nc.scalar, sem("s_act"))
        DV = Queue(nc.vector, sem("s_dve"))
        PO = Queue(nc.gpsimd, sem("s_pool"))
        SP = Queue(nc.sync, sem("s_sp"))

        x_sb = sb("x_sb", [128, KC, B * S])
        c_sb = sb("c_sb", [128, EC, S])
        chi = sb("chi", [128, EC, S], F32R)
        clo = sb("clo", [128, EC, S], F32R)
        wq = sb("wq", [128, 2, KC, C], F32R)
        wo = sb("wo", [128, 2, KC, C], F32R)
        wki = sb("wki", [128, 2, EC, C], F32R)
        wvi = sb("wvi", [128, 2, EC, C], F32R)
        wk = sb("wk", [128, 2, EC, C], F32R)
        wv = sb("wv", [128, 2, EC, C], F32R)
        bo = [sb(f"bo{l}", [128, KC]) for l in range(2)]
        ident = sb("ident", [128, 128])
        ones = sb("ones", [128, 128])
        mhalf = sb("mhalf", [128, 2 * H])
        fmask = sb("fmask", [128, 2])
        hmask = sb("hmask", [128, KC, H])
        ind = sb("ind", [4, 2, KT], F32R)
        big = sb("big", [H, S], F32R)
        QP = sb("QP", [128, H, S], F32R)
        KP = sb("KP", [128, H, KT], F32R)
        qhi = sb("qhi", [128, KC, S], F32R)
        qlo = sb("qlo", [128, KC, S], F32R)
        khi = sb("khi", [128, KC, KT], F32R)
        klo = sb("klo", [128, KC, KT], F32R)
        VX = [sb(f"VX{i}", [128, VW]) for i in range(3)]
        VY = [sb(f"VY{i}", [128, 2, VW]) for i in range(3)]
        VXh = [v[:, 0:H * VS].rearrange("p (h r) -> p h r", r=VS) for v in VX]
        VYh = [v[:, :, 0:H * VS].rearrange("p c (h r) -> p c h r", r=VS) for v in VY]
        P = sb("P", [128, PR, 2, S])
        Y = sb("Y", [128, PR, 2, S])
        y21 = sb("y21", [128, 32])
        ln2 = sb("ln2", [128, 1])
        flat = lambda a: a[:, :, :, :].rearrange("p a b c -> p (a b c)")
        G = [flat(wk)[:, 0:896], flat(wk)[:, 896:1792], flat(wv)[:, 0:896]]
        PH = [flat(wv)[:, 896 + 512 * i:896 + 512 * i + 512].rearrange("p (c s) -> p c s", c=2) for i in range(HR)]
        Vs = [sb(f"Vs{i}", [128, 512]) for i in range(2)]
        O2 = sb("O2", [128, 2, 2, C])
        O = [O2[:, i] for i in range(2)]
        rs = sb("rs", [128, 4, 4])
        ta = sb("ta", [128, 2, 64])
        tb = sb("tb", [128, 2, 64])
        ahi = sb("ahi", [128, KC, S], F32R)
        alo = sb("alo", [128, 2, S], F32R)
        m_sb = sb("m_sb", [128, 2, 2 * H])
        mhi = sb("mhi", [2 * H, S], F32R)
        mlo = sb("mlo", [2 * H, S], F32R)
        ipS = [sb(f"ipS{i}", [128, 2, H, NIP]) for i in range(3)]
        ST = sb("ST", [128, 2, H, 6])
        cip = sb("cip", [128, EC, B * NIP])
        csq = sb("csq", [128, EC, B * NIP])
        kip = sb("kip", [128, KC, B * NIP])
        vhi = sb("vhi", [128, KC, B * NIP], F32R)
        vlo = sb("vlo", [128, KC, B * NIP], F32R)
        invip = sb("invip", [128, B * NIP])
        nrm = sb("nrm", [128, B * NIP])
        bdh = sb("bdh", [128, KC, H, NIP], F32R)
        bdl = sb("bdl", [128, KC, H, NIP], F32R)
        Mb = sb("Mb", [H * NIP, C])
        e2 = sb("e2", [128, 2, H])
        n2 = sb("n2", [128, 2, H])
        rn = sb("rn", [128, 2, H])
        t1 = sb("t1", [128, 2, H, NIP])
        t2 = f1 = f2 = t1
        ex = sb("ex", [128, 2, H, NIP])
        mx = sb("mx", [128, 2, H])
        sm = sb("sm", [128, 2, H])
        ri = sb("ri", [128, 2, H])
        rm = sb("rm", [128, 2, H])
        w4 = sb("w4", [128, 2, H, NIP])
        wT = sb("wT", [H * NIP, S])

        def stage(tile, at, n):
            return flat(tile)[:, at:at + n * C].rearrange("p (k n) -> p k n", n=C)

        sq0, sk0 = stage(Y, 0, KC), stage(Y, KC * C, EC)
        ski0, sv0, svi0 = stage(P, 0, EC), stage(P, EC * C, EC), stage(O2, 0, EC)
        so0 = stage(Y, 0, KC)
        wki1, wvi1 = stage(Y, 0, EC), stage(Y, EC * C, EC)
        sq1, sk1, sv1 = stage(Y, 0, KC), stage(Y, KC * C, EC), stage(Y, 0, EC)
        so1 = c_sb[:, :, :].rearrange("p k s -> p (k s)")[:, 0:KC * C].rearrange("p (k n) -> p k n", n=C)
        ind_f = flat(Y)[0:4, 2240:2240 + 2 * KT].rearrange("p (l t) -> p l t", l=2)
        big_f = flat(Y)[0:H, 2240 + 2 * KT:2240 + 2 * KT + S]

        S1 = Bank(ps("pS1"))
        S2 = [Bank(ps(f"pS2{i}")) for i in range(2)]
        PV = Bank(ps("pPV"))
        GP = [Bank(ps(f"pGP{i}")) for i in range(2)]
        MI = [Bank(ps(f"pMI{i}")) for i in range(2)]
        step = [-1]
        turn = [0, 0]

        def misc(line):
            turn[line] += 1
            return GP[1] if line and step[0] < B - 1 and turn[line] % 2 else MI[line]

        qd = [nc.dram_tensor(f"qd{u}", (2, C, S), F32, kind="Internal").ap() for u in range(U)]
        kd = [nc.dram_tensor(f"kd{u}", (2, C, KT), F32, kind="Internal").ap() for u in range(U)]

        l_x = [Landing(sem(f"l_x{b}")) for b in range(B)]
        l_c = Landing(sem("l_c"))
        l_w = {n: Landing(sem(f"l_w_{n}")) for n in
               ("q0", "k0", "ki0", "v0", "vi0", "o0", "q1", "k1", "v1", "o1", "ip1", "const", "row", "ind0", "ind1", "ind8", "ind9")}
        l_st = {(a, i): Landing(sem(f"l_st{a}{i}")) for a in "qk" for i in range(2)}
        l_ld = [[Landing(sem(f"l_ld{i}{g}")) for g in range(NG)] for i in range(2)]
        l_m = [Landing(sem(f"l_m{i}")) for i in range(2)]
        l_out = Landing(sem("l_out"))

        def load(dst, src, landing):
            s = landing.add()
            SP.do(call(nc.sync.dma_start, dst, src), s)
            return landing.all()

        def load320(dst, src, landing, lo, n):
            load(dst[:, 0:2, lo:lo + n], src[0:256, lo:lo + n].rearrange("(c p) n -> p c n", p=128), landing)
            return load(dst[0:64, 2, lo:lo + n], src[256:320, lo:lo + n], landing)

        def load512(dst, src, landing):
            return load(dst, src.rearrange("(c p) n -> p c n", p=128), landing)

        def load_twice(dst, src, landing):
            load(dst[64:128, 2, :], src[256:320, :], landing)
            return load320(dst, src, landing, 0, C)

        w_ready, t_w = {}, {}
        ip_read = [None]
        c_ready, c_split, c_free = {}, {}, {}

        def load_ctx(u):
            SP.wait(c_split.get(u - 1), w_ready.get("o1") if u == B + 4 else None)
            c_ready[u] = load512(c_sb[:, :, :], cT[:, (u % B) * S:(u % B) * S + S], l_c)

        def split(W, src, landed, *freed, lo=None):
            E_ = lo or PO
            AC.wait(landed, *freed)
            t = AC.sig(call(nc.scalar.activation, W[:, 0], src, ACT.Copy))
            E_.wait(t, landed, *freed)
            return E_.sig(call(E_.engine.tensor_tensor, W[:, 1], src, W[:, 0].bitcast(F32), ALU.subtract))

        x_ready = {}
        t_q0 = load_twice(sq0, Wq0, l_w["q0"])
        x_ready[0] = load320(x_sb, xT, l_x[0], 0, S)
        load_ctx(0)
        t_k0 = load512(sk0, Wk0, l_w["k0"])
        t_ki0 = load512(ski0, Wki0, l_w["ki0"])
        t_v0 = load512(sv0, Wv0, l_w["v0"])
        t_vi0 = load512(svi0, Wvi0, l_w["vi0"])
        load(ident[:, :], ident_d, l_w["const"])
        load(ind_f, ind_d, l_w["const"])
        load(hmask[:, :, :], hm_d, l_w["const"])
        load(fmask[:, :], fs, l_w["const"])
        load(bo[0][:, :], bo0, l_w["const"])
        load(bo[1][:, :], bo1, l_w["const"])
        consts = load512(cip[:, :, :], cipT, l_w["const"])
        for b in range(1, B):
            x_ready[b] = load320(x_sb, xT, l_x[b], b * S, S)

        w_ready["q0"] = split(wq, sq0, t_q0, lo=DV)

        def split_rest():
            w_ready["k0"] = split(wk, sk0, t_k0, lo=DV)
            w_ready["ki0"] = split(wki, ski0, t_ki0)
            w_ready["v0"] = split(wv, sv0, t_v0, lo=DV)
            w_ready["vi0"] = split(wvi, svi0, t_vi0)

        big_f_set = DV.sig(call(nc.vector.memset, big_f, 30000.0))
        AC.wait(consts)
        ind_ready = AC.sig(call(nc.scalar.activation, ind[:, :, :], ind_f, ACT.Copy))
        DV.sig(call(nc.vector.memset, ones[:, :], 1.0))
        mh_set = PO.sig(call(nc.gpsimd.memset, mhalf[:, :], -0.5))
        PO.wait(mh_set)
        DV.sig(call(nc.vector.memset, ln2[:, :], float(np.log(2.0))))
        DV.sig(call(nc.vector.memset, y21[:, :], 0.0))
        y21_zero = (DV.sem, DV.n)
        DV.wait(y21_zero)
        ones_set = DV.sig(call(nc.vector.memset, y21[:, 21:22], 1.0))
        for i in range(3):
            DV.sig(call(nc.vector.memset, VX[i][:, :], 0.0))
            z = DV.sig(call(nc.vector.memset, VY[i][:, :, :], 0.0))
            DV.wait(z)
            DV.sig(call(nc.vector.memset, VXh[i][:, :, 16:17], 1.0))
            DV.sig(call(nc.vector.memset, VYh[i][:, 1, :, 16:17], 1.0))
            z = DV.sig(call(nc.vector.memset, VYh[i][64:128, 0, :, 16:17], 1.0))
            DV.wait(z)
            DV.sig(call(nc.vector.memset, VYh[i][64:TXT0, 0, :, 16:17], 0.0))
        v_set = (DV.sem, DV.n)
        DV.sig(call(nc.vector.memset, khi[:, :, S:KT].bitcast(F32), 0.0))
        k_zero = DV.sig(call(nc.vector.memset, klo[:, :, S:KT].bitcast(F32), 0.0))
        AC.wait(big_f_set)
        big_ready = AC.sig(call(nc.scalar.activation, big[:, :], big_f, ACT.Copy))

        x1_ready = {}
        st_done = {}
        ld_done = {}
        s2_done = {}
        m_ready = {}
        v_ready = {}
        g_ready = {}
        mb_ready = {}
        kip_ready = [None]
        vip_ready = [None]
        invip_ready = [None]
        pv_done = {}
        gp_read = {}
        Vs_free = {}
        O_free = {}
        st = {"q": None, "k": None, "ST": None, "aT": None,
              "m": [], "mT": None, "wT": None, "bd": None, "ind": {}}

        def products(out, pairs, ns):
            for n, (l, r) in enumerate(pairs):
                fn = call(nc.tensor.matmul, out, l, r, start=(n == 0), stop=(n == len(pairs) - 1))
                if n == len(pairs) - 1:
                    mark = PE.sig(fn)
                else:
                    PE.do(fn)
                if n % 3 == 2:
                    yield 3 * ns
            return mark

        def pairs320(W, m0, M, hi, lo):
            ms = slice(m0, m0 + M)
            out = []
            for k in range(2):
                out += [(W[:, 0, k, ms], hi[:, k, 0:S]), (W[:, 0, k, ms], lo[:, k, 0:S]), (W[:, 1, k, ms], hi[:, k, 0:S])]
            return out + [(W[:, 0, 2, ms], hi[:, 2, 0:S]), (W[0:64, 1, 2, ms], hi[0:64, 2, 0:S])]

        def pairs512(W, ms, ts):
            out = []
            for k in range(EC):
                out += [(W[:, 0, k, ms], chi[:, k, ts]), (W[:, 0, k, ms], clo[:, k, ts]), (W[:, 1, k, ms], chi[:, k, ts])]
            return out

        x_split, q_read = {}, {}

        def split_x(u):
            L, b = divmod(u, B)
            ready = (x_ready if L == 0 else x1_ready)[b]
            cols = slice(b * S, b * S + S)
            AC.wait(ready, st["k"], k_zero, q_read.get(u - 1))
            for k in range(KC):
                K = CHUNK[k]
                t = AC.sig(call(nc.scalar.activation, khi[0:K, k, 0:S], x_sb[0:K, k, cols], ACT.Copy))
                E_ = PO if k < 2 else DV
                E_.wait(t, ready, st["k"], k_zero, q_read.get(u - 1))
                dst = klo[:, k, 0:S] if k < 2 else khi[64:128, 2, 0:S]
                lo = E_.sig(call(E_.engine.tensor_tensor, dst, x_sb[0:K, k, cols], khi[0:K, k, 0:S].bitcast(F32), ALU.subtract))
                x_split.setdefault(u, []).append(lo)
                yield 150

        def split_c(u):
            for k in range(EC):
                AC.wait(c_ready[u], c_free.get(u - 1))
                t = AC.sig(call(nc.scalar.activation, chi[:, k, :], c_sb[:, k, :], ACT.Copy))
                PO.wait(t, c_ready[u], c_free.get(u - 1))
                c_split[u] = PO.sig(call(nc.gpsimd.tensor_tensor, clo[:, k, :], c_sb[:, k, :], chi[:, k, :].bitcast(F32), ALU.subtract))
                yield 150
            if u == B + 3:
                SP.wait(c_split[u])
                t_w["o1"] = load_twice(so1, Wo1, l_w["o1"])
                behind.append(("o1", swap_out()))
            elif u + 1 < U:
                load_ctx(u + 1)

        def swap_out():
            w_ready["o1"] = split(wo, so1, t_w["o1"], st["aT"])
            load_ctx(B + 4)
            yield

        def store(u, which, part, th, tl):
            hi, lo = (qhi, qlo) if which == "q" else (khi, klo)
            dram = (qd if which == "q" else kd)[u]
            W = S if which == "q" else KT
            land = l_st[(which, u % 2)]
            M, cs = (128, slice(0, 2)) if part == 0 else (64, slice(2, 3))
            for z, (tile, tok) in enumerate(((hi, th), (lo, tl))):
                if part == 0:
                    d_ap = dram[z, 0:256, :].rearrange("(c p) n -> p c n", p=128)
                else:
                    d_ap = dram[z, 256:320, :].rearrange("(c p) n -> p c n", p=64)
                s = land.add()
                SP.wait(tok, k_zero)
                SP.do(call(nc.sync.dma_start, d_ap, tile[0:M, cs, 0:W].bitcast(F32)), s)
            if part == 1:
                st[which] = st_done[(u, which)] = land.all()

        def high_low(done, hi, lo, src, *free, more=()):
            AC.wait(done, *free)
            for h_, _, s_ in ((hi, lo, src), *more):
                th = AC.sig(call(nc.scalar.activation, h_, s_, ACT.Copy))
            DV.wait(done, th, *free)
            for h_, l_, s_ in ((hi, lo, src), *more):
                tl = DV.sig(call(nc.vector.tensor_tensor, l_, s_, h_.bitcast(F32), ALU.subtract))
            return th, tl

        def queries(u):
            L = u // B
            for part, chunks in enumerate(((0, 1), (2,))):
                bank = misc(1)
                PE.wait(*bank.free)
                PE.wait(w_ready[f"q{L}"], *x_split[u])
                for n, m in enumerate(chunks):
                    done = yield from products(bank.ap[0:CHUNK[m], n * S:n * S + S],
                                               pairs320(wq, 128 * m, CHUNK[m], khi, klo), 112)
                q_read[u] = done
                M, cs = CHUNK[chunks[0]], slice(chunks[0], chunks[-1] + 1)
                src = bank.ap[0:M, 0:len(chunks) * S].rearrange("p (c s) -> p c s", s=S)
                th, tl = high_low(done, qhi[0:M, cs, :], qlo[0:M, cs, :], src, st["q"])
                bank.free = [th, tl]
                store(u, "q", part, th, tl)
                yield 600 if u >= B else 50

        def keys(u):
            L, b = divmod(u, B)
            free = (st["k"], k_zero, q_read[u])
            if L == 0:
                bank = misc(1)
                PE.wait(*bank.free)
                PE.wait(w_ready["k0"], c_split[u])
                for m in range(KC):
                    done = yield from products(bank.ap[0:CHUNK[m], 78 * m:78 * m + 78],
                                               pairs512(wk, slice(128 * m, 128 * m + CHUNK[m]), slice(0, 78)), 90)
                t0 = high_low(done, khi[:, 0:2, 0:TXT0], klo[:, 0:2, 0:TXT0],
                              bank.ap[:, 0:156].rearrange("p (c t) -> p c t", c=2)[:, :, 0:TXT0], *free,
                              more=[(khi[0:64, 2, 0:TXT0], klo[0:64, 2, 0:TXT0], bank.ap[0:64, 156:156 + TXT0])])
                bank.free = list(t0)
                yield 600 if u >= B else 50
            for part, chunks in enumerate(((0, 1), (2,))):
                bank = misc(1)
                PE.wait(*bank.free)
                PE.wait(w_ready["k1" if L else "ki0"], c_split[u])
                lo = 0 if L else TXT0 - 1
                for n, m in enumerate(chunks):
                    done = yield from products(bank.ap[0:CHUNK[m], n * S + lo:n * S + S],
                                               pairs512(wki, slice(128 * m, 128 * m + CHUNK[m]), slice(lo, S)), 112)
                M, cs = CHUNK[chunks[0]], slice(chunks[0], chunks[-1] + 1)
                src = bank.ap[0:M, 0:len(chunks) * S].rearrange("p (c s) -> p c s", s=S)
                if L == 0:
                    th, tl = high_low(done, khi[0:M, cs, TXT0:S], klo[0:M, cs, TXT0:S], src[:, :, TXT0:S], *free)
                    bank.free = [th, tl]
                else:
                    th, tl = high_low(done, khi[0:M, cs, NIP:S], klo[0:M, cs, NIP:S], src[:, :, 0:TXT1], *free)
                    bank.free = [th, tl]
                    th, tl = high_low(kip_ready[0], khi[0:M, cs, 0:NIP], klo[0:M, cs, 0:NIP], kip[0:M, cs, NIP * b:NIP * b + NIP])
                store(u, "k", part, th, tl)
                yield 600 if u >= B else 50

        def load_pack(u, g):
            base, land = BASE[u % 2], l_ld[u % 2][g]
            SP.wait(st_done[(u, "q")], st_done[(u, "k")], s2_done.get((u - 2, g)))
            hs = slice(4 * g, 4 * g + 4)
            for z, row in ((0, 0), (0, 16), (1, 32)):
                src = qd[u][z, 64 * g:64 * g + 64, :].rearrange("(h d) s -> d h s", d=D)
                s = land.add()
                SP.do(call(nc.sync.dma_start, QP[base + row:base + row + D, hs, :].bitcast(F32), src), s)
            for z, row in ((0, 0), (1, 16), (0, 32)):
                src = kd[u][z, 64 * g:64 * g + 64, :].rearrange("(h d) s -> d h s", d=D)
                s = land.add()
                SP.do(call(nc.sync.dma_start, KP[base + row:base + row + D, hs, :].bitcast(F32), src), s)
            ld_done[(u, g)] = land.all()

        def load_ind(u):
            base, L = BASE[u % 2], u // B
            SP.wait(ind_ready, s2_done.get((u - 2, NG - 1)))
            for h in range(0, H, 4):
                s = l_w[f"ind{u}"].add()
                SP.do(call(nc.sync.dma_start, KP[base + ROWS:base + SROWS, h:h + 4, :].bitcast(F32),
                                                      ind[:, L, None, :].to_broadcast([4, 4, KT]).bitcast(F32)), s)
            st["ind"][u] = l_w[f"ind{u}"].all()
            if L == 1:
                SP.wait(big_ready)
                for r in (50, 51):
                    s = l_w[f"ind{u}"].add()
                    SP.do(call(nc.sync.dma_start, QP[base + r:base + r + 1, :, :].bitcast(F32), big[:, :].bitcast(F32)), s)
                st["ind"][u] = l_w[f"ind{u}"].all()

        def values(u):
            L, b = divmod(u, B)
            i = u % 3
            tiles = [(None, wv), (0, wvi), (1, wvi)] if L == 0 else [(0, wvi), (1, wvi)]
            old = pv_done.get((u - 3, NG - 1))
            v_ready[u] = []
            for ch, w in tiles:
                bank = misc(1)
                ts = slice(128 * (ch or 0), 128 * (ch or 0) + 128)
                PE.wait(*bank.free)
                PE.wait(w_ready["v1" if L else "v0" if ch is None else "vi0"], c_split[u])
                done = yield from products(bank.ap[:, 0:C], [(c, v) for v, c in pairs512(w, slice(0, C), ts)], 140)
                c_free[u] = done
                src = bank.ap[:, 0:C].rearrange("p (h d) -> p h d", d=D)
                AC.wait(done, v_set, old)
                if ch is None:
                    t = AC.sig(call(nc.scalar.activation, VXh[i][0:TXT0, :, 0:D], src[0:TXT0], ACT.Copy))
                    bank.free = [t]
                elif L == 0 and ch == 0:
                    t = AC.sig(call(nc.scalar.activation, VYh[i][64:128, 0, :, 0:D], src[64:128], ACT.Copy))
                    bank.free = [t]
                    DV.wait(t)
                    t = DV.sig(call(nc.vector.memset, VYh[i][64:TXT0, 0, :, 0:D], 0.0))
                else:
                    t = AC.sig(call(nc.scalar.activation, VYh[i][:, ch, :, 0:D], src, ACT.Copy))
                    bank.free = [t]
                v_ready[u].append(t)
                yield 600 if u >= B else 50

        def gram(u):
            i = u % 3
            g_ready[u] = []
            for ch in range(2):
                bank = misc(1)
                ts = slice(128 * ch, 128 * ch + 128)
                PE.wait(*bank.free)
                PE.wait(c_split[u])
                pairs = []
                for k in range(EC):
                    pairs += [(chi[:, k, ts], chi[:, k, :]), (chi[:, k, ts], clo[:, k, :]), (clo[:, k, ts], chi[:, k, :])]
                done = yield from products(bank.ap[:, 0:S], pairs, 112)
                c_free[u] = done
                free = (gp_read.get(u - 3), c_free[B - 1])
                hi = G[i][:, 256 * ch:256 * ch + 256]
                AC.wait(done, *free)
                th = AC.sig(call(nc.scalar.activation, hi, bank.ap[:, 0:S], ACT.Copy))
                n = 128 if ch == 0 else 256
                lo = G[i][:, 512 + 128 * ch:512 + 128 * ch + n]
                DV.wait(done, th, *free)
                tl = DV.sig(call(nc.vector.tensor_tensor, lo, bank.ap[:, 0:n], hi[:, 0:n].bitcast(F32), ALU.subtract))
                if ch:
                    DV.wait(tl)
                    tl = DV.sig(call(nc.vector.tensor_scalar, lo[:, 0:128], lo[:, 0:128].bitcast(F32), 2.0, None, ALU.mult))
                g_ready[u] += [th, tl]
                DV.wait(done, th, v_set, pv_done.get((u - 3, NG - 1)))
                z = DV.sig(call(nc.vector.tensor_copy, VYh[i][:, ch, :, 16:20],
                                bank.ap[:, None, TXT1:S].to_broadcast([128, H, NIP])))
                if u < B + 3:
                    DV.wait(z)
                    z = DV.sig(call(nc.vector.memset, VYh[i][:, ch, :, 20:21], 1.0))
                bank.free = [th, tl, z]
                v_ready[u].append(z)
                yield 600 if u >= B else 50

        def ip_prep():
            for w, dst, name in ((wki1, kip, "k"), (wvi1, None, "v")):
                bank = misc(1)
                PE.wait(*bank.free)
                PE.wait(w_ready["ip1"], consts)
                for m in range(KC):
                    M = CHUNK[m]
                    for k in range(EC):
                        fn = (call(nc.tensor.matmul,
                            bank.ap[0:M, 32 * m:32 * m + 32], w[:, k, m * 128:m * 128 + M], cip[:, k, :],
                            start=(k == 0), stop=(k == EC - 1)))
                        done = PE.sig(fn) if (m == 2 and k == EC - 1) else PE.do(fn)
                    yield 500
                ip_read[0] = done
                two = bank.ap[:, 0:64].rearrange("p (c n) -> p c n", n=32)
                last = bank.ap[0:64, 64:96]
                if name == "k":
                    AC.wait(done)
                    AC.sig(call(nc.scalar.activation, kip[:, 0:2, :], two, ACT.Copy))
                    kip_ready[0] = AC.sig(call(nc.scalar.activation, kip[0:64, 2, :], last, ACT.Copy))
                    bank.free = [kip_ready[0]]
                else:
                    bank.free = list(high_low(done, vhi[:, 0:2, :], vlo[:, 0:2, :], two,
                                              more=[(vhi[0:64, 2, :], vlo[0:64, 2, :], last)]))
                    vip_ready[0] = bank.free[1]
                yield 50
            DV.wait(consts)
            sq = DV.sig(call(nc.vector.tensor_tensor, csq[:, :, :], cip[:, :, :], cip[:, :, :], ALU.mult))
            yield 600
            bank = misc(1)
            PE.wait(*bank.free)
            PE.wait(sq, ones_set)
            for k in range(EC):
                fn = (call(nc.tensor.matmul, bank.ap[:, 0:32], ones[:, :], csq[:, k, :],
                                              start=(k == 0), stop=(k == EC - 1)))
                done = PE.sig(fn) if k == EC - 1 else PE.do(fn)
            yield 600
            DV.wait(done)
            z = DV.sig(call(nc.vector.tensor_scalar, nrm[:, :], bank.ap[:, 0:32], 1e-24, None, ALU.max))
            bank.free = [z]
            PO.wait(z)
            SP.wait(ip_read[0])
            t_w["q1"] = load_twice(sq1, Wq1, l_w["q1"])
            t_w["k1"] = load512(sk1, Wk1, l_w["k1"])
            invip_ready[0] = PO.sig(call(nc.gpsimd.tensor_tensor, invip[:, :], nrm[:, :], mhalf[:, 0:B * NIP], ALU.pow))
            yield 600

        def ip_values(u):
            b = u % B
            DV.wait(vip_ready[0], consts, st["bd"])
            full = lambda v, k: v[0:CHUNK[k], k, None, NIP * b:NIP * b + NIP].bitcast(F32).to_broadcast([CHUNK[k], H, NIP])
            for v, dst in ((vhi, bdh), (vlo, bdl)):
                for k in range(KC):
                    K = CHUNK[k]
                    t = DV.sig(call(nc.vector.tensor_tensor, dst[0:K, k], full(v, k),
                                    hmask[0:K, k, :, None].to_broadcast([K, H, NIP]), ALU.mult))
            yield
            bank = misc(0)
            PE.wait(*bank.free)
            PE.wait(t, w_ready["o1"])
            pairs = []
            for k in range(KC):
                K = CHUNK[k]
                h_, l_ = (v[0:K, k].rearrange("p h n -> p (h n)") for v in (bdh, bdl))
                pairs += [(h_, wo[0:K, 0, k, :]), (h_, wo[0:K, 1, k, :]), (l_, wo[0:K, 0, k, :])]
            done = yield from products(bank.ap[0:H * NIP, 0:C], pairs, 140)
            st["bd"] = done
            yield
            AC.wait(done, x1_ready.get(("out", u - 1)))
            mb_ready[u] = AC.sig(call(nc.scalar.activation, Mb[:, :], bank.ap[0:H * NIP, 0:C], ACT.Copy))
            bank.free = [mb_ready[u]]
            yield

        def split_all(u):
            yield from split_x(u)
            if u == B:
                w_ready["q1"] = split(wq, sq1, t_w["q1"], q_read[B - 1])
            yield from split_c(u)
            if u == B:
                w_ready["k1"] = split(wki, sk1, t_w["k1"], c_free[B - 1])
                SP.wait(w_ready["q1"], w_ready["k1"])
                t_w["v1"] = load512(sv1, Wv1, l_w["v1"])

        def prepare(u):
            yield from queries(u)
            yield from keys(u)
            if u == B:
                w_ready["v1"] = split(wvi, sv1, t_w["v1"], c_free[B - 1])
            yield from values(u)
            if u >= B:
                yield from gram(u)
            if u + 1 < U:
                yield from split_all(u + 1)

        ip_copied = {}

        def score_max(u, h):
            L, base = u // B, BASE[u % 2]
            bank = GP[0] if h % 2 and step[0] < B - 1 else S1
            PE.wait(ld_done[(u, h // 4)], *bank.free)
            for sc in range(2):
                fn = (call(nc.tensor.matmul, bank.ap[:, sc * S:sc * S + S],
                                                QP[base:base + ROWS, h, sc * 128:sc * 128 + 128],
                                                KP[base:base + ROWS, h, 0:S], start=True, stop=True))
                done = PE.sig(fn) if sc else PE.do(fn)
            v = bank.ap[:, :].rearrange("p (c t) -> p c t", c=2)
            DV.wait(done, *st["m"])
            if L == 0:
                DV.sig(call(nc.vector.tensor_reduce, m_sb[:, :, h], v[:, :, 0:TXT0], AX, ALU.max))
                t = DV.sig(call(nc.vector.tensor_reduce, m_sb[:, :, H + h], v[:, :, TXT0:S], AX, ALU.max))
                bank.free = [t]
            else:
                t = DV.sig(call(nc.vector.tensor_reduce, m_sb[:, :, h], v[:, :, NIP:S], AX, ALU.max))
                DV.wait(x1_ready.get(("ip", u - 3)))
                t2_ = DV.sig(call(nc.vector.tensor_copy, ipS[u % 3][:, :, h, :], v[:, :, 0:NIP]))
                bank.free = [t, t2_]
                ip_copied[u] = t2_
            m_ready[u] = t

        def shift_rows(u):
            L, base = u // B, BASE[u % 2]
            R = 2 * H if L == 0 else H
            bank = S1
            PE.wait(*bank.free)
            PE.wait(m_ready[u], consts)
            for sc in range(2):
                fn = (call(nc.tensor.transpose, bank.ap[0:R, sc * 128:sc * 128 + 128], m_sb[:, sc, 0:R], ident[:, :]))
                done = PE.sig(fn) if sc else PE.do(fn)
            st["m"] = [done]
            AC.wait(done, st["mT"])
            th = AC.sig(call(nc.scalar.activation, mhi[0:R, :], bank.ap[0:R, 0:S], ACT.Copy))
            DV.wait(done, th, st["mT"])
            tl = DV.sig(call(nc.vector.tensor_tensor, mlo[0:R, :], bank.ap[0:R, 0:S], mhi[0:R, :].bitcast(F32), ALU.subtract))
            bank.free = [th, tl]
            SP.wait(th, s2_done.get((u - 2, NG - 1)))
            rows = [(48, mhi, 0), (50, mhi, H), (49, mlo, 0), (51, mlo, H)] if L == 0 else [(48, mhi, 0), (49, mlo, 0)]
            for r, tile, h0 in rows:
                if tile is mlo:
                    SP.wait(tl)
                s = l_m[u % 2].add()
                SP.do(call(nc.sync.dma_start, 
                    QP[base + r:base + r + 1, :, :].bitcast(F32), tile[h0:h0 + H, :].bitcast(F32)), s)
            m_ready[u] = st["mT"] = l_m[u % 2].all()

        exp_done = {}
        y_done, ph_done, w_done, gp_done = {}, {}, {}, {}

        def scores(u, h):
            L, base = u // B, BASE[u % 2]
            off = NIP if L else 0
            n = u * H + h
            bank = S2[n % 2]
            PE.wait(m_ready[u], ld_done[(u, h // 4)], st["ind"][u if u < 2 else (B + u % 2 if L else u % 2)], *bank.free)
            for ch in range(2):
                fn = (call(nc.tensor.matmul, bank.ap[:, ch * S:ch * S + S],
                                                KP[base:base + SROWS, h, off + ch * 128:off + ch * 128 + 128],
                                                QP[base:base + SROWS, h, :], start=True, stop=True))
                done = PE.sig(fn) if ch else PE.do(fn)
            if h % 4 == 3:
                s2_done[(u, h // 4)] = done
            p = n % PR
            src = bank.ap[:, :].rearrange("p (c s) -> p c s", c=2)
            pv_free = pv_done.get(((n - PR) // H, ((n - PR) % H) // 4))
            if L:
                AC.wait(done, gp_done.get(n - HR), w_done.get(n - HR), c_free[B - 1])
                ph_done[n] = AC.sig(call(nc.scalar.activation, PH[n % HR], src, ACT.Exp, scale=0.25))
            AC.wait(done, pv_free, w_ready["ki0"], w_ready["v0"], ones_set)
            twice = {"bias": ln2[:, 0:1]} if L else {}
            exp_done[n] = AC.sig(call(nc.scalar.activation, P[:, p, :, :], src, ACT.Exp, scale=0.25, **twice))
            bank.free = [exp_done[n]]
            if L:
                PO.wait(exp_done[n], ph_done[n], pv_free, w_ready["k1"], w_ready["v1"])
                w_done[n] = PO.sig(call(nc.gpsimd.tensor_tensor, Y[:, p, :, :], P[:, p, :, :], PH[n % HR].bitcast(F32), ALU.subtract))

        def quad(u, h):
            n, i = u * H + h, u % 3
            p = n % PR
            bank = GP[n % 2]
            ph = PH[n % HR]
            PE.wait(ph_done[n], *g_ready[u])
            PE.wait(*bank.free)
            jobs = [(0, 0, 0), (512, 0, 0), (256, 1, 0), (640, 1, 0), (128, 0, 1), (384, 1, 1), (768, 1, 1)]
            for k, (col, src, dst) in enumerate(jobs):
                fn = call(nc.tensor.matmul, bank.ap[:, dst * S:dst * S + S], G[i][:, col:col + 128], ph[:, src, :],
                          start=(k in (0, 4)), stop=(k in (3, 6)))
                done = PE.sig(fn) if k == 6 else PE.do(fn)
            gp_read[u] = gp_done[n] = done
            DV.wait(done, w_done[n])
            t = DV.sig(call(nc.vector.tensor_tensor, Y[:, p, :, :], bank.ap[:, :].rearrange("p (c s) -> p c s", c=2),
                            Y[:, p, :, :], ALU.mult))
            bank.free = [t]
            y_done[n] = t

        vs_done = {}

        def weigh(u, g):
            L, i = u // B, u % 3
            last = u * H + 4 * g + 3
            PE.wait(exp_done[last], *v_ready[u])
            PE.wait(*PV.free)
            hs = [(j, 4 * g + j, (u * H + 4 * g + j) % PR) for j in range(4)]
            if L == 0:
                for j, h, p in hs:
                    PE.do(call(nc.tensor.matmul, PV.ap[32 * j:32 * j + 32, 0:S], VX[i][0:TXT0, VS * h:VS * h + 32],
                                                            P[0:TXT0, p, 0, :], start=True, stop=True, tile_position=(0, 32 * j)))
                for ch in range(2):
                    for j, h, p in hs:
                        fn = (call(nc.tensor.matmul, 
                            PV.ap[32 * j:32 * j + 32, S:2 * S], VY[i][:, ch, VS * h:VS * h + 32], P[:, p, ch, :],
                            start=(ch == 0), stop=(ch == 1), tile_position=(0, 32 * j)))
                        done = PE.sig(fn) if ch and j == 3 else PE.do(fn)
            else:
                PE.wait(ones_set)
                for ch in range(2):
                    for j, h, p in hs:
                        PE.do(call(nc.tensor.matmul, 
                            PV.ap[32 * j:32 * j + 32, 0:S], VY[i][:, ch, VS * h:VS * h + 32], P[:, p, ch, :],
                            start=(ch == 0), stop=False, tile_position=(0, 32 * j)))
                PE.wait(y_done[last])
                for ch in range(2):
                    for j, h, p in hs:
                        fn = call(nc.tensor.matmul, PV.ap[32 * j:32 * j + 32, 0:S], y21[:, :], Y[:, p, ch, :],
                                  start=False, stop=(ch == 1), tile_position=(0, 32 * j))
                        done = PE.sig(fn) if ch and j == 3 else PE.do(fn)
            pv_done[(u, g)] = done
            N = 2 * S if L == 0 else S
            k = (u * NG + g) % 2
            AC.wait(done, Vs_free.get(k))
            vs_done[(u, g)] = AC.sig(call(nc.scalar.activation, Vs[k][:, 0:N], PV.ap[:, 0:N], ACT.Copy))
            PV.free = [vs_done[(u, g)]]

        o_done = {}

        def normalize(u, g):
            L, k, i = u // B, (u * NG + g) % 2, u % 2
            nt = 4 if L == 0 else 2
            yield
            bank = misc(0)
            PE.wait(*bank.free)
            PE.wait(vs_done[(u, g)], consts)
            for t in range(nt):
                fn = (call(nc.tensor.transpose, bank.ap[:, 128 * t:128 * t + 128], Vs[k][:, 128 * t:128 * t + 128], ident[:, :]))
                done = PE.sig(fn) if t == nt - 1 else PE.do(fn)
            Vs_free[k] = done
            yield
            v = bank.ap[:, 0:128 * nt].rearrange("p (t j r) -> p t j r", t=nt, j=4)
            od = O[i][:, :, 64 * g:64 * g + 64]
            od4 = od.rearrange("p c (j d) -> p c j d", j=4)
            col = 16 if L == 0 else 20
            DV.wait(done, O_free.get(i), st.get("rs"), w_ready["vi0"])
            tr = DV.sig(call(nc.vector.reciprocal, rs[:, 0:nt, :], v[:, :, :, col]))
            DV.wait(tr)
            if L == 0:
                rb = rs[:, :, :, None].to_broadcast([128, 4, 4, D])
                t_a = DV.sig(call(nc.vector.tensor_tensor, ta[:, :, :].rearrange("p c (j d) -> p c j d", j=4), v[:, 0:2, :, 0:D], rb[:, 0:2], ALU.mult))
                t_b = DV.sig(call(nc.vector.tensor_tensor, tb[:, :, :].rearrange("p c (j d) -> p c j d", j=4), v[:, 2:4, :, 0:D], rb[:, 2:4], ALU.mult))
                bank.free = [t_b]
                DV.wait(t_b)
                st["rs"] = o_done[u] = DV.sig(call(nc.vector.tensor_tensor, od, ta[:, :, :], tb[:, :, :], ALU.add))
            else:
                rb = rs[:, 0:2, :, None].to_broadcast([128, 2, 4, D])
                st["rs"] = o_done[u] = DV.sig(call(nc.vector.tensor_tensor, od4, v[:, :, :, 0:D], rb, ALU.mult))
                DV.wait(st["ST"])
                t = DV.sig(call(nc.vector.tensor_copy, ST[:, :, 4 * g:4 * g + 4, :], v[:, :, :, 16:22]))
                bank.free = [t]
                hs = slice(4 * g, 4 * g + 4)
                DV.wait(t)
                t = DV.sig(call(nc.vector.scalar_tensor_tensor, e2[:, :, hs], ST[:, :, hs, 4], 0.25e-24, ST[:, :, hs, 4], ALU.mult, ALU.mult))
                DV.wait(t)
                t = DV.sig(call(nc.vector.tensor_tensor, n2[:, :, hs], ST[:, :, hs, 5], e2[:, :, hs], ALU.max))
                PO.wait(t, st["ST"])
                st_done[("rn", u)] = PO.sig(call(nc.gpsimd.tensor_tensor, rn[:, :, hs], n2[:, :, hs],
                                                 mhalf[:, 0:8].rearrange("p (c h) -> p c h", c=2), ALU.pow))
            yield

        def finish(u):
            L, b = divmod(u, B)
            i = u % 2
            if L == 1:
                yield from ip_values(u)

                def dv(fn, *w):
                    DV.wait(*w)
                    return DV.sig(fn)
                bc = lambda a: a[:, :, :, None].to_broadcast([128, 2, H, NIP])
                t = dv(call(nc.vector.tensor_tensor, t1[:, :, :, :], ST[:, :, :, 0:NIP], bc(rn), ALU.mult), st_done[("rn", u)])
                st["ST"] = t
                iv = invip[:, None, NIP * b:NIP * b + NIP].to_broadcast([128, 2 * H, NIP])
                t = dv(call(nc.vector.tensor_tensor, t2[:, :, :, :].rearrange("p c h n -> p (c h) n"),
                                                 t1[:, :, :, :].rearrange("p c h n -> p (c h) n"), iv, ALU.mult), t, invip_ready[0])
                yield
                t = dv(call(nc.vector.scalar_tensor_tensor, f1[:, :, :, :], t2[:, :, :, :], 1.0, ipS[u % 3][:, :, :, :], ALU.mult, ALU.add), t, ip_copied[u])
                x1_ready[("ip", u)] = t
                t = dv(call(nc.vector.tensor_reduce, mx[:, :, :], f1[:, :, :, :], AX, ALU.max), t)
                t = dv(call(nc.vector.tensor_tensor, f2[:, :, :, :], f1[:, :, :, :], bc(mx), ALU.subtract), t)
                AC.wait(t)
                ta_ = AC.sig(call(nc.scalar.activation, ex[:, :, :, :], f2[:, :, :, :], ACT.Exp, scale=0.25))
                yield
                t = dv(call(nc.vector.tensor_reduce, sm[:, :, :], ex[:, :, :, :], AX, ALU.add), ta_)
                t = dv(call(nc.vector.reciprocal, ri[:, :, :], sm[:, :, :]), t)
                t = dv(call(nc.vector.tensor_tensor, rm[:, :, :], ri[:, :, :], fmask[:, :, None].to_broadcast([128, 2, H]), ALU.mult), t, consts)
                tw = dv(call(nc.vector.tensor_tensor, w4[:, :, :, :], ex[:, :, :, :], bc(rm), ALU.mult), t)
                yield
            bank = misc(0)
            bank2 = misc(0)
            PE.wait(*bank.free)
            PE.wait(o_done[u], consts)
            for k in range(2):
                for sc in range(2):
                    fn = (call(nc.tensor.transpose, bank.ap[:, k * S + sc * 128:k * S + sc * 128 + 128],
                                                            O[i][:, sc, 128 * k:128 * k + 128], ident[:, :]))
                    done = PE.sig(fn) if k and sc else PE.do(fn)
            tA = high_low(done, ahi[:, 0:2, :], alo[:, :, :], bank.ap[:, :].rearrange("p (c s) -> p c s", c=2), st["aT"])
            bank.free = list(tA)
            yield
            yield
            PE.wait(*bank2.free)
            for sc in range(2):
                fn = (call(nc.tensor.transpose, bank2.ap[0:64, sc * 128:sc * 128 + 128], O[i][:, sc, 256:320], ident[:, :]))
                done2 = PE.sig(fn) if sc else PE.do(fn)
            O_free[i] = done2
            tB = high_low(done2, ahi[0:64, 2, :], ahi[64:128, 2, :], bank2.ap[0:64, 0:S], st["aT"])
            bank2.free = list(tB)
            yield
            if L == 0:
                yield
            if L == 1:
                bank3 = misc(0)
                PE.wait(*bank3.free)
                PE.wait(tw)
                for sc in range(2):
                    fn = (call(nc.tensor.transpose, bank3.ap[0:H * NIP, sc * 128:sc * 128 + 128],
                                                       w4[:, sc, :, :].rearrange("p h n -> p (h n)"), ident[:, :]))
                    done = PE.sig(fn) if sc else PE.do(fn)
                AC.wait(done, st["wT"])
                tW = AC.sig(call(nc.scalar.activation, wT[:, :], bank3.ap[0:H * NIP, 0:S], ACT.Copy))
                bank3.free = [tW]
                yield
            for chunks in ((0, 1), (2,)):
                bank = misc(0)
                PE.wait(*bank.free)
                PE.wait(*tA, *tB, w_ready[f"o{L}"])
                if L == 1:
                    PE.wait(tW, mb_ready[u])
                for n, m in enumerate(chunks):
                    M = CHUNK[m]
                    pairs = pairs320(wo, 128 * m, M, ahi, alo)
                    for k, (l, r) in enumerate(pairs):
                        final = k == len(pairs) - 1 and L == 0
                        fn = call(nc.tensor.matmul, bank.ap[0:M, n * S:n * S + S], l, r, start=(k == 0), stop=final)
                        if final and m == chunks[-1]:
                            done = PE.sig(fn)
                        else:
                            PE.do(fn)
                    if L == 1:
                        fn = (call(nc.tensor.matmul, 
                            bank.ap[0:M, n * S:n * S + S], Mb[:, m * 128:m * 128 + M], wT[:, :], start=False, stop=True))
                        done = PE.sig(fn) if m == chunks[-1] else PE.do(fn)
                yield
                for n, m in enumerate(chunks):
                    M = CHUNK[m]
                    dst = x_sb[0:M, m, b * S:b * S + S]
                    DV.wait(done, x_ready[b], consts)
                    if L == 1:
                        DV.wait(x1_ready[b])
                    t = DV.sig(call(nc.vector.scalar_tensor_tensor, 
                        dst, bank.ap[0:M, n * S:n * S + S], bo[L][0:M, m:m + 1], dst, ALU.add, ALU.add))
                bank.free = [t]
                if L == 1:
                    SP.wait(t)
                    for m in chunks:
                        s = l_out.add()
                        SP.do(call(nc.sync.dma_start, 
                            outT[128 * m:128 * m + CHUNK[m], b * S:b * S + S],
                            x_sb[0:CHUNK[m], m, b * S:b * S + S]), s)
                yield
            st["aT"] = st["wT"] = done
            if L == 0:
                x1_ready[b] = t
            else:
                x1_ready[("out", u)] = done

        def drain(*gens):
            for g in gens:
                for _ in g:
                    pass

        ahead, behind = [], []
        credit = [0]

        def advance_ahead(ns):
            credit[0] += ns
            while credit[0] > 0 and ahead:
                try:
                    credit[0] -= next(ahead[0])
                except StopIteration:
                    ahead.pop(0)
            if not ahead:
                credit[0] = 0

        def advance_behind():
            while behind:
                try:
                    if next(behind[0][1]) is None:
                        return
                except StopIteration:
                    behind.pop(0)

        def complete(key):
            while any(k == key for k, _ in behind):
                advance_behind()

        drain(split_all(0))
        split_rest()
        drain(queries(0), keys(0))
        load_ind(0)
        for g in range(NG):
            load_pack(0, g)
        SP.wait(w_ready["q0"])
        t_o0 = load_twice(so0, Wo0, l_w["o0"])
        w_ready["o0"] = split(wo, so0, t_o0)
        SP.wait(w_ready["o0"], w_ready["k0"], ind_ready, big_ready)
        load512(wki1, Wki1, l_w["ip1"])
        w_ready["ip1"] = load512(wvi1, Wvi1, l_w["ip1"])
        ahead += [values(0), split_all(1), prepare(1)]
        for h in range(H):
            score_max(0, h)
            advance_ahead(1000)
        shift_rows(0)
        drain(*ahead)
        ahead.clear()
        load_ind(1)
        for g in range(NG):
            load_pack(1, g)
        scores(0, 0)

        def weigh_behind(u, g):
            s = u * NG + g - 2
            complete((s // NG, s % NG))
            weigh(u, g)
            behind.append(((u, g), normalize(u, g)))
            if g == NG - 1:
                behind.append((("end", u), finish(u)))

        for u in range(U):
            step[0] = u
            if u + 2 < U:
                ahead.append(prepare(u + 2))
            if u == 2:
                ahead.append(ip_prep())
            nxt = loads = 0
            for h in range(H):
                goal = min(H, (3 * (h + 1) + 1) // 2) if u + 1 < U else 0
                if nxt < goal:
                    score_max(u + 1, nxt)
                    nxt += 1
                advance_behind()
                if h == MH and u + 1 < U:
                    shift_rows(u + 1)
                if h + 1 < H:
                    scores(u, h + 1)
                advance_ahead(500)
                if u >= B:
                    quad(u, h)
                advance_behind()
                if nxt < goal:
                    score_max(u + 1, nxt)
                    nxt += 1
                advance_ahead(500)
                if h % 4 == 0 and u * NG + h // 4:
                    weigh_behind(*divmod(u * NG + h // 4 - 1, NG))
                while (u + 2, "k") in st_done and loads < NG and (u, loads) in s2_done:
                    load_pack(u + 2, loads)
                    loads += 1
            if u + 2 < U:
                drain(*ahead)
                ahead.clear()
                while loads < NG:
                    load_pack(u + 2, loads)
                    loads += 1
                if u + 2 in (B, B + 1):
                    load_ind(u + 2)
            if u + 1 < U:
                scores(u + 1, 0)
        weigh_behind(U - 1, NG - 1)
        while behind:
            advance_behind()
        SP.wait(l_out.all())
        for land in list(l_w.values()) + l_x + [l_c]:
            SP.wait(land.all())

        block = ctx.enter_context(nc.Block())
        block.tensor(PE.run)
        block.scalar(AC.run)
        block.vector(DV.run)
        block.sync(SP.run)
        block.gpsimd(PO.run)


def kernel(**inputs):
    import numpy as _np
    import concourse.bacc as _bacc
    from concourse import mybir as _mybir
    from concourse.bass_utils import run_bass_kernel_spmd as _run

    g = {k: _np.asarray(v) for k, v in inputs.items()}
    T = lambda a: _np.ascontiguousarray(a.T)

    def col(v):
        out = _np.zeros((3, 128), v.dtype)
        out[0], out[1], out[2, :64] = v[0:128], v[128:256], v[256:320]
        return T(out)

    ctx = g["ctx_2048"]
    ind = _np.zeros((4, 2, KT), _np.float32)
    ind[0:2, 0, 0:TXT0] = -1.0
    ind[2:4, 0, TXT0:S] = -1.0
    ind[0:2, 1, NIP:S] = -1.0
    ind[2, 1, S:KT] = -1.0
    hm = _np.zeros((128, 3, H), _np.float32)
    for c in range(C):
        hm[c % 128, c // 128, c // D] = 1.0
    arrays = {
        "xT": T(g["x"].reshape(B * S, C)),
        "cT": T(ctx.reshape(B * S, E)),
        "cipT": T(ctx[:, TXT1:, :].reshape(B * NIP, E)),
        "fs": T(g["fside_S_0"].reshape(2, 128)),
        "Wq0": T(g["L0_xattn_Wq"]), "Wk0": T(g["L0_xattn_Wk"]), "Wv0": T(g["L0_xattn_Wv"]),
        "Wki0": T(g["L0_xattn_Wk_ip"]), "Wvi0": T(g["L0_xattn_Wv_ip"]), "Wo0": T(g["L0_xattn_Wo"]),
        "bo0": col(g["L0_xattn_bo"]),
        "Wq1": g["L1_xattn_W_q"], "Wk1": g["L1_xattn_W_k"], "Wv1": g["L1_xattn_W_v"],
        "Wki1": g["L1_xattn_W_k_ip"], "Wvi1": g["L1_xattn_W_v_ip"], "Wo1": g["L1_xattn_W_out"],
        "bo1": col(g["L1_xattn_b_out"]),
        "ident": _np.eye(128, dtype=_np.float32), "ind": ind, "hm": hm,
    }
    nc = _bacc.Bacc("TRN2", target_bir_lowering=False, num_devices=1, dynamic_dma_scratch_size=1024)
    args, feeds = [], {}
    for name, a in arrays.items():
        a = _np.ascontiguousarray(a)
        feeds[f"in_{name}"] = a
        args.append(nc.dram_tensor(f"in_{name}", a.shape, _mybir.dt.from_np(a.dtype), kind="ExternalInput").ap())
    args.append(nc.dram_tensor("out_T", (C, B * S), _mybir.dt.float32, kind="ExternalOutput").ap())
    build(nc, *args)
    r = _run(nc, [feeds], core_ids=[0])
    got = r.results[0]["out_T"]
    return _np.ascontiguousarray(got.T).reshape(B, S, C)
```

```python
from contextlib import ExitStack

import numpy as np

import concourse.bass as bass
from concourse import mybir

F32 = mybir.dt.float32
F32R = mybir.dt.float32r
ALU = mybir.AluOpType
ACT = mybir.ActivationFunctionType
AX = mybir.AxisListType.X

B, S, C, E, H, D = 8, 256, 320, 512, 20, 16
TXT0 = 77
TXT1 = 252
NIP = 4
KC = 3
EC = 4
NG = 5
KT = S + 4
ROWS = 48
SROWS = 52
BASE = (0, 64)
PR = 6
MH = (14, 16)
LEAD = (4, 0)
RATE = (5, 5)
TURN = 10
EVAC = 450
SPLIT = (300, 500)
REST = (2, 2)
EARLY_EVAC = (1, 1)
FREE = 2
QB = 2
YSUM = 0
LH = 11
EARLY = (520, 350)
LATE = (750, 800)
HR = 3
VS = 22
VW = H * VS + 10
CHUNK = (128, 128, 64)


def call(fn, *args, **kwargs):
    return fn, args, kwargs


class Queue:

    def __init__(self, engine, sem):
        self.engine, self.sem, self.n, self.ops, self.met = engine, sem, 0, [], {}

    def wait(self, *marks):
        for m in marks:
            if m is None:
                continue
            sem, value = m
            if self.met.get(id(sem), 0) < value:
                self.met[id(sem)] = value
                self.ops.append((call(self.engine.wait_ge, sem, value), None, 0))

    def do(self, what, sem=None):
        self.ops.append((what, sem, 16))

    def sig(self, what):
        self.n += 1
        self.ops.append((what, self.sem, 1))
        return (self.sem, self.n)

    def run(self, e):
        for (fn, args, kwargs), sem, by in self.ops:
            made = fn(*args, **kwargs)
            if sem is not None:
                made.then_inc(sem, by)


class Landing:

    def __init__(self, sem):
        self.sem, self.n = sem, 0

    def add(self):
        self.n += 16
        return self.sem

    def all(self):
        return (self.sem, self.n)


class Bank:
    given = 0

    def __init__(self, ap):
        self.ap, self.free, self.held, self.at = ap, [], False, 0

    def give(self, marks):
        Bank.given += 1
        self.free, self.held, self.at = list(marks), False, Bank.given


def build(nc, xT, cT, cipT, fs, Wq0, Wk0, Wv0, Wki0, Wvi0, Wo0, bo0,
          Wq1, Wk1, Wv1, Wki1, Wvi1, Wo1, bo1, ident_d, ind_d, hm_d, outT):
    U = 2 * B
    with ExitStack() as ctx:
        def sb(name, shape, dt=F32):
            return ctx.enter_context(nc.sbuf_tensor(name, shape, dt))

        def ps(name):
            return ctx.enter_context(nc.psum_tensor(name, [128, 512], F32))

        def sem(name):
            return ctx.enter_context(nc.semaphore(name))

        PE = Queue(nc.tensor, sem("s_pe"))
        AC = Queue(nc.scalar, sem("s_act"))
        DV = Queue(nc.vector, sem("s_dve"))
        PO = Queue(nc.gpsimd, sem("s_pool"))
        SP = Queue(nc.sync, sem("s_sp"))

        x_sb = sb("x_sb", [128, KC, B * S])
        c_sb = sb("c_sb", [128, EC, S])
        chi = sb("chi", [128, EC, S], F32R)
        clo = sb("clo", [128, EC, S], F32R)
        wq = sb("wq", [128, 2, KC, C], F32R)
        wo = sb("wo", [128, 2, KC, C], F32R)
        wki = sb("wki", [128, 2, EC, C], F32R)
        wvi = sb("wvi", [128, 2, EC, C], F32R)
        wk = sb("wk", [128, 2, EC, C], F32R)
        wv = sb("wv", [128, 2, EC, C], F32R)
        bo = [sb(f"bo{l}", [128, KC]) for l in range(2)]
        ident = sb("ident", [128, 128])
        ones = sb("ones", [128, 128])
        mhalf = sb("mhalf", [128, 2 * H])
        fmask = sb("fmask", [128, 2])
        hmask = sb("hmask", [128, KC, H])
        ind = sb("ind", [4, 2, KT], F32R)
        big = sb("big", [H, S], F32R)
        QP = sb("QP", [128, H, S], F32R)
        KP = sb("KP", [128, H, KT], F32R)
        qhi = sb("qhi", [128, KC, S], F32R)
        qlo = sb("qlo", [128, KC, S], F32R)
        khi = sb("khi", [128, KC, KT], F32R)
        klo = sb("klo", [128, KC, KT], F32R)
        VX = [sb(f"VX{i}", [128, VW]) for i in range(3)]
        VY = [sb(f"VY{i}", [128, 2, VW]) for i in range(3)]
        VXh = [v[:, 0:H * VS].rearrange("p (h r) -> p h r", r=VS) for v in VX]
        VYh = [v[:, :, 0:H * VS].rearrange("p c (h r) -> p c h r", r=VS) for v in VY]
        P = sb("P", [128, PR, 2, S])
        Y = sb("Y", [128, PR, 2, S])
        kt = sb("kt", [128, C])
        y21 = sb("y21", [128, 32])
        ln2 = sb("ln2", [128, 1])
        flat = lambda a: a[:, :, :, :].rearrange("p a b c -> p (a b c)")
        G = [flat(wk)[:, 0:896], flat(wk)[:, 896:1792], flat(wv)[:, 0:896]]
        PH = [flat(wv)[:, 896 + 512 * i:896 + 512 * i + 512].rearrange("p (c s) -> p c s", c=2) for i in range(HR)]
        Vs = [sb(f"Vs{i}", [128, 512]) for i in range(2)]
        O2 = sb("O2", [128, 2, 2, C])
        O = [O2[:, i] for i in range(2)]
        rs = sb("rs", [128, 4, 4])
        ta = sb("ta", [128, 2, 64])
        tb = sb("tb", [128, 2, 64])
        ahi = sb("ahi", [128, KC, S], F32R)
        alo = sb("alo", [128, 2, S], F32R)
        m_sb = sb("m_sb", [128, 2, 2 * H])
        mhi = sb("mhi", [2 * H, S], F32R)
        mlo = sb("mlo", [2 * H, S], F32R)
        ipS = [sb(f"ipS{i}", [128, 2, H, NIP]) for i in range(3)]
        ST = sb("ST", [128, 2, H, 6])
        cip = sb("cip", [128, EC, B * NIP])
        csq = sb("csq", [128, EC, B * NIP])
        kip = sb("kip", [128, KC, B * NIP])
        vhi = sb("vhi", [128, KC, B * NIP], F32R)
        vlo = sb("vlo", [128, KC, B * NIP], F32R)
        invip = sb("invip", [128, B * NIP])
        nrm = sb("nrm", [128, B * NIP])
        bdh = sb("bdh", [128, KC, H, NIP], F32R)
        bdl = sb("bdl", [128, KC, H, NIP], F32R)
        Mb = sb("Mb", [H * NIP, C])
        e2 = sb("e2", [128, 2, H])
        n2 = sb("n2", [128, 2, H])
        rn = sb("rn", [128, 2, H])
        t1 = sb("t1", [128, 2, H, NIP])
        t2 = f1 = f2 = t1
        ex = sb("ex", [128, 2, H, NIP])
        mx = sb("mx", [128, 2, H])
        sm = sb("sm", [128, 2, H])
        ri = sb("ri", [128, 2, H])
        rm = sb("rm", [128, 2, H])
        w4 = sb("w4", [128, 2, H, NIP])
        wT = sb("wT", [H * NIP, S])

        def stage(tile, at, n):
            return flat(tile)[:, at:at + n * C].rearrange("p (k n) -> p k n", n=C)

        sq0, sk0 = stage(Y, 0, KC), stage(Y, KC * C, EC)
        ski0, sv0, svi0 = stage(P, 0, EC), stage(P, EC * C, EC), stage(O2, 0, EC)
        so0 = stage(Y, 0, KC)
        wki1, wvi1 = stage(Y, 0, EC), stage(Y, EC * C, EC)
        sq1, sk1 = stage(Y, 0, KC), stage(Y, KC * C, EC)
        sv1 = stage(Y, 0, KC), stage(Y, (KC + EC) * C, 1)
        so1 = c_sb[:, :, :].rearrange("p k s -> p (k s)")[:, 0:KC * C].rearrange("p (k n) -> p k n", n=C)
        ind_f = flat(P)[0:4, 2 * EC * C:2 * EC * C + KT], flat(Y)[0:4, 2 * EC * C:2 * EC * C + KT]
        big_f = kt[0:H, 0:S]

        S1 = Bank(ps("pS1"))
        S2 = [Bank(ps(f"pS2{i}")) for i in range(2)]
        PV = Bank(ps("pPV"))
        GP = [Bank(ps(f"pGP{i}")) for i in range(QB)]
        MI = [Bank(ps(f"pMI{i}")) for i in range(4 - QB)]
        step = [-1]

        def take():
            pool = [b for b in [S1, *MI] + (GP if step[0] < B - 1 else []) if not b.held]
            bank = min(pool, key=lambda b: b.at)
            bank.held = True
            return bank

        qd = [nc.dram_tensor(f"qd{u}", (3, D, H, S), F32, kind="Internal").ap() for u in range(U)]
        kd = [nc.dram_tensor(f"kd{u}", (3, D, H, KT), F32, kind="Internal").ap() for u in range(U)]

        l_x = [Landing(sem(f"l_x{b}")) for b in range(B)]
        l_c = Landing(sem("l_c"))
        l_w = {n: Landing(sem(f"l_w_{n}")) for n in
               ("ident", "q0", "k0", "ki0", "v0", "vi0", "o0", "q1", "k1", "v1", "o1", "ip1", "const", "row", "ind0", "ind1", "ind8", "ind9")}
        l_st = {(a, i): Landing(sem(f"l_st{a}{i}")) for a in "qk" for i in range(2)}
        l_ld = [[Landing(sem(f"l_ld{i}{g}")) for g in range(NG)] for i in range(2)]
        l_m = [Landing(sem(f"l_m{i}")) for i in range(2)]
        l_out = Landing(sem("l_out"))

        def load(dst, src, landing):
            s = landing.add()
            SP.do(call(nc.sync.dma_start, dst, src), s)
            return landing.all()

        def load320(dst, src, landing, lo, n):
            load(dst[:, 0:2, lo:lo + n], src[0:256, lo:lo + n].rearrange("(c p) n -> p c n", p=128), landing)
            return load(dst[0:64, 2, lo:lo + n], src[256:320, lo:lo + n], landing)

        def load512(dst, src, landing):
            return load(dst, src.rearrange("(c p) n -> p c n", p=128), landing)

        def load_twice(dst, src, landing):
            load(dst[64:128, 2, :], src[256:320, :], landing)
            return load320(dst, src, landing, 0, C)

        w_ready, t_w = {}, {}
        ip_read = [None]
        c_ready, c_split, c_free = {}, {}, {}

        def load_ctx(u):
            SP.wait(c_split.get(u - 1), w_ready.get("o1") if u == B + 4 else None)
            c_ready[u] = load512(c_sb[:, :, :], cT[:, (u % B) * S:(u % B) * S + S], l_c)

        def split(W, src, landed, *freed, lo=None, ks=slice(None)):
            E_ = lo or PO
            AC.wait(landed, *freed)
            t = AC.sig(call(nc.scalar.activation, W[:, 0, ks], src, ACT.Copy))
            E_.wait(t, landed, *freed)
            return E_.sig(call(E_.engine.tensor_tensor, W[:, 1, ks], src, W[:, 0, ks].bitcast(F32), ALU.subtract))

        x_ready = {}
        x_ready[0] = load320(x_sb, xT, l_x[0], 0, S)
        t_q0 = load_twice(sq0, Wq0, l_w["q0"])
        load_ctx(0)
        ident_ready = load(ident[:, :], ident_d, l_w["ident"])
        t_k0 = load512(sk0, Wk0, l_w["k0"])
        t_ki0 = load512(ski0, Wki0, l_w["ki0"])
        t_v0 = load512(sv0, Wv0, l_w["v0"])
        t_vi0 = load512(svi0, Wvi0, l_w["vi0"])
        for l in range(2):
            load(ind_f[l], ind_d[:, l, :], l_w["const"])
        load(hmask[:, :, :], hm_d, l_w["const"])
        load(fmask[:, :], fs, l_w["const"])
        load(bo[0][:, :], bo0, l_w["const"])
        load(bo[1][:, :], bo1, l_w["const"])
        consts = load512(cip[:, :, :], cipT, l_w["const"])
        for b in range(1, B):
            x_ready[b] = load320(x_sb, xT, l_x[b], b * S, S)

        def split_rest():
            w_ready["k0"] = split(wk, sk0, t_k0, lo=DV)
            w_ready["ki0"] = split(wki, ski0, t_ki0, lo=DV)
            w_ready["v0"] = split(wv, sv0, t_v0)
            w_ready["vi0"] = split(wvi, svi0, t_vi0)

        mh_set = PO.sig(call(nc.gpsimd.memset, mhalf[:, :], -0.5))
        PO.wait(mh_set)
        DV.sig(call(nc.vector.memset, khi[:, :, S:KT].bitcast(F32), 0.0))
        k_zero = DV.sig(call(nc.vector.memset, klo[:, :, S:KT].bitcast(F32), 0.0))
        set_up = {}

        def constants():
            big_f_set = DV.sig(call(nc.vector.memset, big_f, 30000.0))
            DV.sig(call(nc.vector.memset, ones[:, :], 1.0))
            DV.sig(call(nc.vector.memset, ln2[:, :], float(np.log(2.0))))
            DV.wait(DV.sig(call(nc.vector.memset, y21[:, :], 0.0)))
            set_up["ones"] = DV.sig(call(nc.vector.memset, y21[:, 21:22], 1.0))
            for i in range(3):
                DV.sig(call(nc.vector.memset, VX[i][:, :], 0.0))
                DV.wait(DV.sig(call(nc.vector.memset, VY[i][:, :, :], 0.0)))
                DV.sig(call(nc.vector.memset, VXh[i][:, :, 16:17], 1.0))
                DV.sig(call(nc.vector.memset, VYh[i][:, 1, :, 16:17], 1.0))
                DV.wait(DV.sig(call(nc.vector.memset, VYh[i][64:128, 0, :, 16:17], 1.0)))
                set_up["v"] = DV.sig(call(nc.vector.memset, VYh[i][64:TXT0, 0, :, 16:17], 0.0))
            AC.wait(consts, big_f_set)
            for l in range(2):
                set_up["ind"] = AC.sig(call(nc.scalar.activation, ind[:, l, :], ind_f[l], ACT.Copy))
            set_up["big"] = AC.sig(call(nc.scalar.activation, big[:, :], big_f, ACT.Copy))

        x1_ready = {}
        st_done = {}
        ld_done = {}
        s2_done = {}
        m_ready = {}
        v_ready = {}
        g_ready = {}
        mb_ready = {}
        kip_ready = [None]
        vip_ready = [None]
        invip_ready = [None]
        pv_done = {}
        gp_read = {}
        Vs_free = {}
        O_free = {}
        st = {"q": None, "k": None, "ST": None, "kt": None, "aT": None,
              "m": [], "mT": None, "wT": None, "bd": None, "ind": {}}

        def products(out, pairs, ns):
            for n, (l, r) in enumerate(pairs):
                fn = call(nc.tensor.matmul, out, l, r, start=(n == 0), stop=(n == len(pairs) - 1))
                if n == len(pairs) - 1:
                    mark = PE.sig(fn)
                else:
                    PE.do(fn)
                if n % 3 == 2:
                    yield 3 * ns
            return mark

        def pairs320(W, m0, M, hi, lo):
            ms = slice(m0, m0 + M)
            out = []
            for k in range(2):
                out += [(W[:, 0, k, ms], hi[:, k, 0:S]), (W[:, 0, k, ms], lo[:, k, 0:S]), (W[:, 1, k, ms], hi[:, k, 0:S])]
            return out + [(W[:, 0, 2, ms], hi[:, 2, 0:S]), (W[0:64, 1, 2, ms], hi[0:64, 2, 0:S])]

        def pairs512(W, ms, ts):
            out = []
            for k in range(EC):
                out += [(W[:, 0, k, ms], chi[:, k, ts]), (W[:, 0, k, ms], clo[:, k, ts]), (W[:, 1, k, ms], chi[:, k, ts])]
            return out

        x_split, q_read = {}, {}

        def split_x(u):
            L, b = divmod(u, B)
            ready = (x_ready if L == 0 else x1_ready)[b]
            cols = slice(b * S, b * S + S)
            AC.wait(ready, st["k"], k_zero, q_read.get(u - 1))
            for k in range(KC):
                K = CHUNK[k]
                t = AC.sig(call(nc.scalar.activation, khi[0:K, k, 0:S], x_sb[0:K, k, cols], ACT.Copy))
                E_ = PO if k < 2 and 0 < u < B + 2 else DV
                E_.wait(t, ready, st["k"], k_zero, q_read.get(u - 1))
                dst = klo[:, k, 0:S] if k < 2 else khi[64:128, 2, 0:S]
                lo = E_.sig(call(E_.engine.tensor_tensor, dst, x_sb[0:K, k, cols], khi[0:K, k, 0:S].bitcast(F32), ALU.subtract))
                x_split.setdefault(u, []).append(lo)
                yield SPLIT[u >= B + 2]

        def split_c(u):
            for k in range(EC):
                AC.wait(c_ready[u], c_free.get(u - 1))
                t = AC.sig(call(nc.scalar.activation, chi[:, k, :], c_sb[:, k, :], ACT.Copy))
                E_ = PO if u < B + 2 else DV
                E_.wait(t, c_ready[u], c_free.get(u - 1))
                c_split[u] = E_.sig(call(E_.engine.tensor_tensor, clo[:, k, :], c_sb[:, k, :], chi[:, k, :].bitcast(F32), ALU.subtract))
                yield SPLIT[u >= B + 2]
            if u < 2 and u + 1 < U:
                load_ctx(u + 1)
            if u == B + 3:
                SP.wait(c_split[u])
                t_w["o1"] = load_twice(so1, Wo1, l_w["o1"])
                behind.append(("o1", swap_out()))

        def swap_out():
            for _ in range(6):
                yield
            w_ready["o1"] = split(wo, so1, t_w["o1"], st["aT"])
            load_ctx(B + 4)
            yield

        def store(u, which, part, th, tl):
            hi, lo = (qhi, qlo) if which == "q" else (khi, klo)
            dram = (qd if which == "q" else kd)[u]
            W = S if which == "q" else KT
            land = l_st[(which, u % 2)]
            planes = ((hi, th, 0), (hi, th, 2), (lo, tl, 1)) if which == "q" else ((hi, th, 0), (hi, th, 1), (lo, tl, 2))
            for tile, tok, z in planes:
                SP.wait(tok, k_zero)
                for m in (0, 1) if part == 0 else (2,):
                    s = land.add()
                    SP.do(call(nc.sync.dma_start, dram[z, :, 8 * m:8 * m + CHUNK[m] // D].rearrange("d h s -> h d s"), tile[0:CHUNK[m], m, 0:W].bitcast(F32)), s)
            if part == 1:
                st[which] = st_done[(u, which)] = land.all()

        def high_low(done, hi, lo, src, *free, more=()):
            AC.wait(done, *free)
            for h_, _, s_ in ((hi, lo, src), *more):
                th = AC.sig(call(nc.scalar.activation, h_, s_, ACT.Copy))
            DV.wait(done, th, *free)
            for h_, l_, s_ in ((hi, lo, src), *more):
                tl = DV.sig(call(nc.vector.tensor_tensor, l_, s_, h_.bitcast(F32), ALU.subtract))
            return th, tl

        def queries(u):
            L = u // B
            for part, chunks in enumerate(((0, 1), (2,))):
                bank = take()
                PE.wait(*bank.free)
                PE.wait(w_ready[f"q{L}"], *x_split[u])
                for n, m in enumerate(chunks):
                    done = yield from products(bank.ap[0:CHUNK[m], n * S:n * S + S],
                                               pairs320(wq, 128 * m, CHUNK[m], khi, klo), 112)
                q_read[u] = done
                yield EVAC
                M, cs = CHUNK[chunks[0]], slice(chunks[0], chunks[-1] + 1)
                src = bank.ap[0:M, 0:len(chunks) * S].rearrange("p (c s) -> p c s", s=S)
                th, tl = high_low(done, qhi[0:M, cs, :], qlo[0:M, cs, :], src, st["q"])
                bank.give([th, tl])
                store(u, "q", part, th, tl)
                yield 50

        def keys(u):
            L, b = divmod(u, B)
            free = (st["k"], k_zero, q_read[u])
            if L == 0:
                bank = take()
                PE.wait(*bank.free)
                PE.wait(w_ready["k0"], c_split[u])
                done = yield from products(bank.ap[:, 0:C], [(c, w) for w, c in pairs512(wk, slice(0, C), slice(0, 128))], 140)
                yield EVAC
                AC.wait(done, st["kt"], set_up["big"])
                t = AC.sig(call(nc.scalar.activation, kt[0:TXT0, :], bank.ap[0:TXT0, 0:C], ACT.Copy))
                bank.give([t])
                yield EVAC
                bank = take()
                PE.wait(*bank.free)
                PE.wait(t, ident_ready)
                for m in range(KC):
                    fn = call(nc.tensor.transpose, bank.ap[0:CHUNK[m], 78 * m:78 * m + TXT0],
                              kt[0:TXT0, 128 * m:128 * m + CHUNK[m]], ident[0:TXT0, 0:TXT0])
                    done = PE.sig(fn) if m == KC - 1 else PE.do(fn)
                st["kt"] = done
                yield EVAC
                t0 = high_low(done, khi[:, 0:2, 0:TXT0], klo[:, 0:2, 0:TXT0],
                              bank.ap[:, 0:156].rearrange("p (c t) -> p c t", c=2)[:, :, 0:TXT0], *free,
                              more=[(khi[0:64, 2, 0:TXT0], klo[0:64, 2, 0:TXT0], bank.ap[0:64, 156:156 + TXT0])])
                bank.give(list(t0))
                yield 50
            for part, chunks in enumerate(((0, 1), (2,))):
                bank = take()
                PE.wait(*bank.free)
                PE.wait(w_ready["k1" if L else "ki0"], c_split[u])
                lo = 0 if L else TXT0 - 1
                for n, m in enumerate(chunks):
                    done = yield from products(bank.ap[0:CHUNK[m], n * S + lo:n * S + S],
                                               pairs512(wki, slice(128 * m, 128 * m + CHUNK[m]), slice(lo, S)), 112)
                yield EVAC
                M, cs = CHUNK[chunks[0]], slice(chunks[0], chunks[-1] + 1)
                src = bank.ap[0:M, 0:len(chunks) * S].rearrange("p (c s) -> p c s", s=S)
                if L == 0:
                    th, tl = high_low(done, khi[0:M, cs, TXT0:S], klo[0:M, cs, TXT0:S], src[:, :, TXT0:S], *free)
                    bank.give([th, tl])
                else:
                    th, tl = high_low(done, khi[0:M, cs, NIP:S], klo[0:M, cs, NIP:S], src[:, :, 0:TXT1], *free)
                    bank.give([th, tl])
                    th, tl = high_low(kip_ready[0], khi[0:M, cs, 0:NIP], klo[0:M, cs, 0:NIP], kip[0:M, cs, NIP * b:NIP * b + NIP])
                store(u, "k", part, th, tl)
                yield 50

        def load_pack(u, g):
            base, land = BASE[u % 2], l_ld[u % 2][g]
            SP.wait(st_done[(u, "q")], st_done[(u, "k")], s2_done.get((u - 2, g)))
            hs = slice(4 * g, 4 * g + 4)
            for pack, dram in ((QP, qd), (KP, kd)):
                src = dram[u][:, :, hs].rearrange("z d h s -> (z d) h s")
                dst = pack[base:base + ROWS, hs, :]
                s = land.add()
                SP.do(call(nc.sync.dma_start, dst.bitcast(F32), src), s)
            ld_done[(u, g)] = land.all()

        def load_ind(u):
            base, L = BASE[u % 2], u // B
            SP.wait(set_up["ind"], s2_done.get((u - 2, NG - 1)))
            for h in range(0, H, 4):
                s = l_w[f"ind{u}"].add()
                SP.do(call(nc.sync.dma_start, KP[base + ROWS:base + SROWS, h:h + 4, :].bitcast(F32),
                                                      ind[:, L, None, :].to_broadcast([4, 4, KT]).bitcast(F32)), s)
            st["ind"][u] = l_w[f"ind{u}"].all()
            if L == 1:
                SP.wait(set_up["big"])
                for r in (50, 51):
                    s = l_w[f"ind{u}"].add()
                    SP.do(call(nc.sync.dma_start, QP[base + r:base + r + 1, :, :].bitcast(F32), big[:, :].bitcast(F32)), s)
                st["ind"][u] = l_w[f"ind{u}"].all()

        def values(u):
            L, b = divmod(u, B)
            i = u % 3
            tiles = [(None, wv), (0, wvi), (1, wvi)] if L == 0 else [(0, wvi), (1, wvi)]
            old = pv_done.get((u - 3, NG - 1))
            v_ready[u] = []
            for ch, w in tiles:
                bank = take()
                ts = slice(128 * (ch or 0), 128 * (ch or 0) + 128)
                PE.wait(*bank.free)
                PE.wait(w_ready["v1" if L else "v0" if ch is None else "vi0"], c_split[u])
                done = yield from products(bank.ap[:, 0:C], [(c, v) for v, c in pairs512(w, slice(0, C), ts)], 140)
                c_free[u] = done
                yield EVAC
                src = bank.ap[:, 0:C].rearrange("p (h d) -> p h d", d=D)
                AC.wait(done, set_up["v"], old)
                if ch is None:
                    t = AC.sig(call(nc.scalar.activation, VXh[i][0:TXT0, :, 0:D], src[0:TXT0], ACT.Copy))
                    bank.give([t])
                elif L == 0 and ch == 0:
                    t = AC.sig(call(nc.scalar.activation, VYh[i][64:128, 0, :, 0:D], src[64:128], ACT.Copy))
                    bank.give([t])
                    DV.wait(t)
                    t = DV.sig(call(nc.vector.memset, VYh[i][64:TXT0, 0, :, 0:D], 0.0))
                else:
                    t = AC.sig(call(nc.scalar.activation, VYh[i][:, ch, :, 0:D], src, ACT.Copy))
                    bank.give([t])
                v_ready[u].append(t)
                yield 50

        def gram(u):
            i = u % 3
            g_ready[u] = []
            for ch in range(2):
                bank = take()
                ts = slice(128 * ch, 128 * ch + 128)
                PE.wait(*bank.free)
                PE.wait(c_split[u])
                pairs = []
                for k in range(EC):
                    pairs += [(chi[:, k, ts], chi[:, k, :]), (chi[:, k, ts], clo[:, k, :]), (clo[:, k, ts], chi[:, k, :])]
                done = yield from products(bank.ap[:, 0:S], pairs, 112)
                c_free[u] = done
                yield EVAC
                free = (gp_read.get(u - 3), c_free[B - 1])
                hi = G[i][:, 256 * ch:256 * ch + 256]
                AC.wait(done, *free)
                th = AC.sig(call(nc.scalar.activation, hi, bank.ap[:, 0:S], ACT.Copy))
                n = 128 if ch == 0 else 256
                lo = G[i][:, 512 + 128 * ch:512 + 128 * ch + n]
                DV.wait(done, th, *free)
                tl = DV.sig(call(nc.vector.tensor_tensor, lo, bank.ap[:, 0:n], hi[:, 0:n].bitcast(F32), ALU.subtract))
                if ch:
                    DV.wait(tl)
                    tl = DV.sig(call(nc.vector.tensor_scalar, lo[:, 0:128], lo[:, 0:128].bitcast(F32), 2.0, None, ALU.mult))
                g_ready[u] += [th, tl]
                DV.wait(done, th, set_up["v"], pv_done.get((u - 3, NG - 1)))
                z = DV.sig(call(nc.vector.tensor_copy, VYh[i][:, ch, :, 16:20],
                                bank.ap[:, None, TXT1:S].to_broadcast([128, H, NIP])))
                if u < B + 3:
                    DV.wait(z)
                    z = DV.sig(call(nc.vector.memset, VYh[i][:, ch, :, 20:21], 1.0))
                bank.give([th, tl, z])
                v_ready[u].append(z)
                yield 50

        def ip_prep():
            for w, dst, name in ((wki1, kip, "k"), (wvi1, None, "v")):
                bank = take()
                PE.wait(*bank.free)
                PE.wait(w_ready["ip1"], consts)
                for m in range(KC):
                    M = CHUNK[m]
                    for k in range(EC):
                        fn = (call(nc.tensor.matmul,
                            bank.ap[0:M, 32 * m:32 * m + 32], w[:, k, m * 128:m * 128 + M], cip[:, k, :],
                            start=(k == 0), stop=(k == EC - 1)))
                        done = PE.sig(fn) if (m == 2 and k == EC - 1) else PE.do(fn)
                    yield 500
                ip_read[0] = done
                two = bank.ap[:, 0:64].rearrange("p (c n) -> p c n", n=32)
                last = bank.ap[0:64, 64:96]
                if name == "k":
                    AC.wait(done)
                    AC.sig(call(nc.scalar.activation, kip[:, 0:2, :], two, ACT.Copy))
                    kip_ready[0] = AC.sig(call(nc.scalar.activation, kip[0:64, 2, :], last, ACT.Copy))
                    bank.give([kip_ready[0]])
                else:
                    bank.give(high_low(done, vhi[:, 0:2, :], vlo[:, 0:2, :], two,
                                       more=[(vhi[0:64, 2, :], vlo[0:64, 2, :], last)]))
                    vip_ready[0] = bank.free[1]
                yield 50
            DV.wait(consts)
            sq = DV.sig(call(nc.vector.tensor_tensor, csq[:, :, :], cip[:, :, :], cip[:, :, :], ALU.mult))
            yield 600
            bank = take()
            PE.wait(*bank.free)
            PE.wait(sq, set_up["ones"])
            for k in range(EC):
                fn = (call(nc.tensor.matmul, bank.ap[:, 0:32], ones[:, :], csq[:, k, :],
                                              start=(k == 0), stop=(k == EC - 1)))
                done = PE.sig(fn) if k == EC - 1 else PE.do(fn)
            yield 600
            DV.wait(done)
            z = DV.sig(call(nc.vector.tensor_scalar, nrm[:, :], bank.ap[:, 0:32], 1e-24, None, ALU.max))
            bank.give([z])
            PO.wait(z)
            invip_ready[0] = PO.sig(call(nc.gpsimd.tensor_tensor, invip[:, :], nrm[:, :], mhalf[:, 0:B * NIP], ALU.pow))
            yield 600

        def ip_values(u):
            b = u % B
            DV.wait(vip_ready[0], consts, st["bd"])
            full = lambda v, k: v[0:CHUNK[k], k, None, NIP * b:NIP * b + NIP].bitcast(F32).to_broadcast([CHUNK[k], H, NIP])
            for v, dst in ((vhi, bdh), (vlo, bdl)):
                for k in range(KC):
                    K = CHUNK[k]
                    t = DV.sig(call(nc.vector.tensor_tensor, dst[0:K, k], full(v, k),
                                    hmask[0:K, k, :, None].to_broadcast([K, H, NIP]), ALU.mult))
                    if k == 1:
                        yield
                yield
            bank = take()
            PE.wait(*bank.free)
            PE.wait(t, w_ready["o1"])
            pairs = []
            for k in range(KC):
                K = CHUNK[k]
                h_, l_ = (v[0:K, k].rearrange("p h n -> p (h n)") for v in (bdh, bdl))
                pairs += [(h_, wo[0:K, 0, k, :]), (h_, wo[0:K, 1, k, :]), (l_, wo[0:K, 0, k, :])]
            done = yield from products(bank.ap[0:H * NIP, 0:C], pairs, 140)
            st["bd"] = done
            yield
            AC.wait(done, x1_ready.get(("out", u - 1)))
            mb_ready[u] = AC.sig(call(nc.scalar.activation, Mb[:, :], bank.ap[0:H * NIP, 0:C], ACT.Copy))
            bank.give([mb_ready[u]])
            yield

        def split_all(u):
            yield from split_x(u)
            yield from split_c(u)
            if u == B:
                w_ready["k1"] = split(wki, sk1, t_w["k1"], c_free[B - 1])
                yield 500
                w_ready["v1"] = split(wvi, sv1[0], t_w["v1"], c_free[B - 1], ks=slice(0, KC))
                w_ready["v1"] = split(wvi, sv1[1], t_w["v1"], c_free[B - 1], ks=slice(KC, EC))

        def prepare(u):
            yield from queries(u)
            if u == B - 1:
                w_ready["q1"] = split(wq, sq1, t_w["q1"], q_read[u])
            yield from keys(u)
            if u == B - 1:
                SP.wait(w_ready["q1"])
                load(sv1[0], Wv1[0:KC * 128].rearrange("(c p) n -> p c n", p=128), l_w["v1"])
                t_w["v1"] = load(sv1[1], Wv1[KC * 128:].rearrange("(c p) n -> p c n", p=128), l_w["v1"])
            yield from values(u)
            if u >= B:
                yield from gram(u)
            if u + 1 < U:
                yield from split_all(u + 1)

        ip_copied = {}

        def score_max(u, h):
            L, base = u // B, BASE[u % 2]
            bank = take()
            PE.wait(ld_done[(u, h // 4)], *bank.free)
            for sc in range(2):
                fn = (call(nc.tensor.matmul, bank.ap[:, sc * S:sc * S + S],
                                                QP[base:base + ROWS, h, sc * 128:sc * 128 + 128],
                                                KP[base:base + ROWS, h, 0:S], start=True, stop=True))
                done = PE.sig(fn) if sc else PE.do(fn)
            v = bank.ap[:, :].rearrange("p (c t) -> p c t", c=2)
            DV.wait(done, *st["m"])
            if L == 0:
                DV.sig(call(nc.vector.tensor_reduce, m_sb[:, :, h], v[:, :, 0:TXT0], AX, ALU.max))
                t = DV.sig(call(nc.vector.tensor_reduce, m_sb[:, :, H + h], v[:, :, TXT0:S], AX, ALU.max))
                bank.give([t])
            else:
                t = DV.sig(call(nc.vector.tensor_reduce, m_sb[:, :, h], v[:, :, NIP:S], AX, ALU.max))
                DV.wait(x1_ready.get(("ip", u - 3)))
                t2_ = DV.sig(call(nc.vector.tensor_copy, ipS[u % 3][:, :, h, :], v[:, :, 0:NIP]))
                bank.give([t, t2_])
                ip_copied[u] = t2_
            m_ready[u] = t

        def shift_rows(u):
            L, base = u // B, BASE[u % 2]
            R = 2 * H if L == 0 else H
            bank = take()
            PE.wait(*bank.free)
            PE.wait(m_ready[u], consts)
            for sc in range(2):
                fn = (call(nc.tensor.transpose, bank.ap[0:R, sc * 128:sc * 128 + 128], m_sb[:, sc, 0:R], ident[:, :]))
                done = PE.sig(fn) if sc else PE.do(fn)
            st["m"] = [done]
            AC.wait(done, st["mT"])
            th = AC.sig(call(nc.scalar.activation, mhi[0:R, :], bank.ap[0:R, 0:S], ACT.Copy))
            DV.wait(done, th, st["mT"])
            tl = DV.sig(call(nc.vector.tensor_tensor, mlo[0:R, :], bank.ap[0:R, 0:S], mhi[0:R, :].bitcast(F32), ALU.subtract))
            bank.give([th, tl])
            SP.wait(th, s2_done.get((u - 2, NG - 1)))
            rows = [(48, mhi, 0), (50, mhi, H), (49, mlo, 0), (51, mlo, H)] if L == 0 else [(48, mhi, 0), (49, mlo, 0)]
            for r, tile, h0 in rows:
                if tile is mlo:
                    SP.wait(tl)
                s = l_m[u % 2].add()
                SP.do(call(nc.sync.dma_start, 
                    QP[base + r:base + r + 1, :, :].bitcast(F32), tile[h0:h0 + H, :].bitcast(F32)), s)
            m_ready[u] = st["mT"] = l_m[u % 2].all()

        exp_done = {}
        y_done, ph_done, w_done, gp_done = {}, {}, {}, {}

        def scores(u, h):
            L, base = u // B, BASE[u % 2]
            off = NIP if L else 0
            n = u * H + h
            bank = S2[n % len(S2)]
            PE.wait(m_ready[u], ld_done[(u, h // 4)], st["ind"][u if u < 2 else (B + u % 2 if L else u % 2)], *bank.free)
            for ch in range(2):
                fn = (call(nc.tensor.matmul, bank.ap[:, ch * S:ch * S + S],
                                                KP[base:base + SROWS, h, off + ch * 128:off + ch * 128 + 128],
                                                QP[base:base + SROWS, h, :], start=True, stop=True))
                done = PE.sig(fn) if ch else PE.do(fn)
            if h % 4 == 3:
                s2_done[(u, h // 4)] = done
            p = n % PR
            src = bank.ap[:, :].rearrange("p (c s) -> p c s", c=2)
            pv_free = pv_done.get(((n - PR) // H, ((n - PR) % H) // 4))
            if L:
                AC.wait(done, gp_done.get(n - HR), w_done.get(n - HR), c_free[B - 1])
                ph_done[n] = AC.sig(call(nc.scalar.activation, PH[n % HR], src, ACT.Exp, scale=0.25))
            AC.wait(done, pv_free, w_ready["ki0"], w_ready["v0"], set_up["ones"])
            twice = {"bias": ln2[:, 0:1]} if L else {}
            exp_done[n] = AC.sig(call(nc.scalar.activation, P[:, p, :, :], src, ACT.Exp, scale=0.25, **twice))
            bank.free = [exp_done[n]]
            if L:
                PO.wait(exp_done[n], ph_done[n], pv_free, w_ready["k1"], w_ready["v1"])
                w_done[n] = PO.sig(call(nc.gpsimd.tensor_tensor, Y[:, p, :, :], P[:, p, :, :], PH[n % HR].bitcast(F32), ALU.subtract))

        def quad(u, h):
            n, i = u * H + h, u % 3
            p = n % PR
            bank = GP[n % len(GP)]
            ph = PH[n % HR]
            PE.wait(ph_done[n], *g_ready[u])
            PE.wait(*bank.free)
            jobs = [(0, 0, 0), (512, 0, 0), (256, 1, 0), (640, 1, 0), (128, 0, 1), (384, 1, 1), (768, 1, 1)]
            for k, (col, src, dst) in enumerate(jobs):
                fn = call(nc.tensor.matmul, bank.ap[:, dst * S:dst * S + S], G[i][:, col:col + 128], ph[:, src, :],
                          start=(k in (0, 4)), stop=(k in (3, 6)))
                done = PE.sig(fn) if k == 6 else PE.do(fn)
            gp_read[u] = gp_done[n] = done

        def quad_y(u, h):
            n = u * H + h
            p = n % PR
            bank = GP[n % len(GP)]
            DV.wait(gp_done[n], w_done[n])
            t = DV.sig(call(nc.vector.tensor_tensor, Y[:, p, :, :], bank.ap[:, :].rearrange("p (c s) -> p c s", c=2),
                            Y[:, p, :, :], ALU.mult))
            bank.free = [t]
            y_done[n] = t
            if YSUM:
                E_ = PO if YSUM == 1 else DV
                E_.wait(t)
                y_done[n] = E_.sig(call(E_.engine.tensor_tensor, Y[:, p, 0, :], Y[:, p, 0, :], Y[:, p, 1, :], ALU.add))

        vs_done = {}

        def weigh(u, g):
            L, i = u // B, u % 3
            last = u * H + 4 * g + 3
            PE.wait(exp_done[last], *v_ready[u])
            PE.wait(*PV.free)
            hs = [(j, 4 * g + j, (u * H + 4 * g + j) % PR) for j in range(4)]
            if L == 0:
                for j, h, p in hs:
                    PE.do(call(nc.tensor.matmul, PV.ap[32 * j:32 * j + 32, 0:S], VX[i][0:TXT0, VS * h:VS * h + 32],
                                                            P[0:TXT0, p, 0, :], start=True, stop=True, tile_position=(0, 32 * j)))
                for ch in range(2):
                    for j, h, p in hs:
                        fn = (call(nc.tensor.matmul, 
                            PV.ap[32 * j:32 * j + 32, S:2 * S], VY[i][:, ch, VS * h:VS * h + 32], P[:, p, ch, :],
                            start=(ch == 0), stop=(ch == 1), tile_position=(0, 32 * j)))
                        done = PE.sig(fn) if ch and j == 3 else PE.do(fn)
            else:
                PE.wait(set_up["ones"])
                for ch in range(2):
                    for j, h, p in hs:
                        PE.do(call(nc.tensor.matmul, 
                            PV.ap[32 * j:32 * j + 32, 0:S], VY[i][:, ch, VS * h:VS * h + 32], P[:, p, ch, :],
                            start=(ch == 0), stop=False, tile_position=(0, 32 * j)))
                PE.wait(y_done[last])
                for ch in range(1 if YSUM else 2):
                    for j, h, p in hs:
                        fn = call(nc.tensor.matmul, PV.ap[32 * j:32 * j + 32, 0:S], y21[:, :], Y[:, p, ch, :],
                                  start=False, stop=(ch == 1 or YSUM > 0), tile_position=(0, 32 * j))
                        done = PE.sig(fn) if j == 3 and (ch or YSUM) else PE.do(fn)
            pv_done[(u, g)] = done

        def evacuate(u, g):
            N = 2 * S if u < B else S
            k = (u * NG + g) % 2
            AC.wait(pv_done[(u, g)], Vs_free.get(k))
            vs_done[(u, g)] = AC.sig(call(nc.scalar.activation, Vs[k][:, 0:N], PV.ap[:, 0:N], ACT.Copy))
            PV.free = [vs_done[(u, g)]]

        o_done = {}

        def normalize(u, g):
            L, k, i = u // B, (u * NG + g) % 2, u % 2
            nt = 4 if L == 0 else 2
            for _ in range(REST[L]):
                yield
            bank = take()
            PE.wait(*bank.free)
            PE.wait(vs_done[(u, g)], consts)
            for t in range(nt):
                fn = (call(nc.tensor.transpose, bank.ap[:, 128 * t:128 * t + 128], Vs[k][:, 128 * t:128 * t + 128], ident[:, :]))
                done = PE.sig(fn) if t == nt - 1 else PE.do(fn)
            Vs_free[k] = done
            yield
            v = bank.ap[:, 0:128 * nt].rearrange("p (t j r) -> p t j r", t=nt, j=4)
            od = O[i][:, :, 64 * g:64 * g + 64]
            od4 = od.rearrange("p c (j d) -> p c j d", j=4)
            col = 16 if L == 0 else 20
            DV.wait(done, O_free.get(i), st.get("rs"), w_ready["vi0"])
            tr = DV.sig(call(nc.vector.reciprocal, rs[:, 0:nt, :], v[:, :, :, col]))
            DV.wait(tr)
            if L == 0:
                rb = rs[:, :, :, None].to_broadcast([128, 4, 4, D])
                t_a = DV.sig(call(nc.vector.tensor_tensor, ta[:, :, :].rearrange("p c (j d) -> p c j d", j=4), v[:, 0:2, :, 0:D], rb[:, 0:2], ALU.mult))
                t_b = DV.sig(call(nc.vector.tensor_tensor, tb[:, :, :].rearrange("p c (j d) -> p c j d", j=4), v[:, 2:4, :, 0:D], rb[:, 2:4], ALU.mult))
                bank.give([t_b])
                DV.wait(t_b)
                st["rs"] = o_done[u] = DV.sig(call(nc.vector.tensor_tensor, od, ta[:, :, :], tb[:, :, :], ALU.add))
            else:
                rb = rs[:, 0:2, :, None].to_broadcast([128, 2, 4, D])
                st["rs"] = o_done[u] = DV.sig(call(nc.vector.tensor_tensor, od4, v[:, :, :, 0:D], rb, ALU.mult))
                DV.wait(st["ST"])
                t = DV.sig(call(nc.vector.tensor_copy, ST[:, :, 4 * g:4 * g + 4, :], v[:, :, :, 16:22]))
                bank.give([t])
                hs = slice(4 * g, 4 * g + 4)
                DV.wait(t)
                t = DV.sig(call(nc.vector.scalar_tensor_tensor, e2[:, :, hs], ST[:, :, hs, 4], 0.25e-24, ST[:, :, hs, 4], ALU.mult, ALU.mult))
                DV.wait(t)
                t = DV.sig(call(nc.vector.tensor_tensor, n2[:, :, hs], ST[:, :, hs, 5], e2[:, :, hs], ALU.max))
                PO.wait(t, st["ST"])
                st_done[("rn", u)] = PO.sig(call(nc.gpsimd.tensor_tensor, rn[:, :, hs], n2[:, :, hs],
                                                 mhalf[:, 0:8].rearrange("p (c h) -> p c h", c=2), ALU.pow))
            yield

        def finish(u):
            L, b = divmod(u, B)
            i = u % 2
            for _ in range(FREE + L):
                yield
            if L == 1:
                def dv(fn, *w):
                    DV.wait(*w)
                    return DV.sig(fn)
                bc = lambda a: a[:, :, :, None].to_broadcast([128, 2, H, NIP])
                t = dv(call(nc.vector.tensor_tensor, t1[:, :, :, :], ST[:, :, :, 0:NIP], bc(rn), ALU.mult), st_done[("rn", u)])
                st["ST"] = t
                iv = invip[:, None, NIP * b:NIP * b + NIP].to_broadcast([128, 2 * H, NIP])
                t = dv(call(nc.vector.tensor_tensor, t2[:, :, :, :].rearrange("p c h n -> p (c h) n"),
                                                 t1[:, :, :, :].rearrange("p c h n -> p (c h) n"), iv, ALU.mult), t, invip_ready[0])
                yield
                t = dv(call(nc.vector.scalar_tensor_tensor, f1[:, :, :, :], t2[:, :, :, :], 1.0, ipS[u % 3][:, :, :, :], ALU.mult, ALU.add), t, ip_copied[u])
                x1_ready[("ip", u)] = t
                yield
                t = dv(call(nc.vector.tensor_reduce, mx[:, :, :], f1[:, :, :, :], AX, ALU.max), t)
                yield
                t = dv(call(nc.vector.tensor_tensor, f2[:, :, :, :], f1[:, :, :, :], bc(mx), ALU.subtract), t)
                yield
                AC.wait(t)
                ta_ = AC.sig(call(nc.scalar.activation, ex[:, :, :, :], f2[:, :, :, :], ACT.Exp, scale=0.25))
                yield
                t = dv(call(nc.vector.tensor_reduce, sm[:, :, :], ex[:, :, :, :], AX, ALU.add), ta_)
                yield
                t = dv(call(nc.vector.reciprocal, ri[:, :, :], sm[:, :, :]), t)
                t = dv(call(nc.vector.tensor_tensor, rm[:, :, :], ri[:, :, :], fmask[:, :, None].to_broadcast([128, 2, H]), ALU.mult), t, consts)
                yield
                tw = dv(call(nc.vector.tensor_tensor, w4[:, :, :, :], ex[:, :, :, :], bc(rm), ALU.mult), t)
                yield
            bank = take()
            PE.wait(*bank.free)
            PE.wait(o_done[u], consts)
            for k in range(2):
                for sc in range(2):
                    fn = (call(nc.tensor.transpose, bank.ap[:, k * S + sc * 128:k * S + sc * 128 + 128],
                                                            O[i][:, sc, 128 * k:128 * k + 128], ident[:, :]))
                    done = PE.sig(fn) if k and sc else PE.do(fn)
            yield
            tA = high_low(done, ahi[:, 0:2, :], alo[:, :, :], bank.ap[:, :].rearrange("p (c s) -> p c s", c=2), st["aT"])
            bank.give(list(tA))
            yield
            yield
            bank2 = take()
            PE.wait(*bank2.free)
            for sc in range(2):
                fn = (call(nc.tensor.transpose, bank2.ap[0:64, sc * 128:sc * 128 + 128], O[i][:, sc, 256:320], ident[:, :]))
                done2 = PE.sig(fn) if sc else PE.do(fn)
            O_free[i] = done2
            yield
            tB = high_low(done2, ahi[0:64, 2, :], ahi[64:128, 2, :], bank2.ap[0:64, 0:S], st["aT"])
            bank2.give(list(tB))
            yield
            if L == 0:
                yield
            if L == 1:
                bank3 = take()
                PE.wait(*bank3.free)
                PE.wait(tw)
                for sc in range(2):
                    fn = (call(nc.tensor.transpose, bank3.ap[0:H * NIP, sc * 128:sc * 128 + 128],
                                                       w4[:, sc, :, :].rearrange("p h n -> p (h n)"), ident[:, :]))
                    done = PE.sig(fn) if sc else PE.do(fn)
                yield
                AC.wait(done, st["wT"])
                tW = AC.sig(call(nc.scalar.activation, wT[:, :], bank3.ap[0:H * NIP, 0:S], ACT.Copy))
                bank3.give([tW])
                yield
            for chunks in ((0, 1), (2,)):
                bank = take()
                PE.wait(*bank.free)
                PE.wait(*tA, *tB, w_ready[f"o{L}"])
                if L == 1:
                    PE.wait(tW, mb_ready[u])
                for n, m in enumerate(chunks):
                    M = CHUNK[m]
                    pairs = pairs320(wo, 128 * m, M, ahi, alo)
                    for k, (l, r) in enumerate(pairs):
                        final = k == len(pairs) - 1 and L == 0
                        fn = call(nc.tensor.matmul, bank.ap[0:M, n * S:n * S + S], l, r, start=(k == 0), stop=final)
                        if final and m == chunks[-1]:
                            done = PE.sig(fn)
                        else:
                            PE.do(fn)
                    if L == 1:
                        fn = (call(nc.tensor.matmul, 
                            bank.ap[0:M, n * S:n * S + S], Mb[:, m * 128:m * 128 + M], wT[:, :], start=False, stop=True))
                        done = PE.sig(fn) if m == chunks[-1] else PE.do(fn)
                yield
                for n, m in enumerate(chunks):
                    M = CHUNK[m]
                    dst = x_sb[0:M, m, b * S:b * S + S]
                    DV.wait(done, x_ready[b], consts)
                    if L == 1:
                        DV.wait(x1_ready[b])
                    t = DV.sig(call(nc.vector.scalar_tensor_tensor, 
                        dst, bank.ap[0:M, n * S:n * S + S], bo[L][0:M, m:m + 1], dst, ALU.add, ALU.add))
                bank.give([t])
                if L == 1:
                    SP.wait(t)
                    for m in chunks:
                        s = l_out.add()
                        SP.do(call(nc.sync.dma_start, 
                            outT[128 * m:128 * m + CHUNK[m], b * S:b * S + S],
                            x_sb[0:CHUNK[m], m, b * S:b * S + S]), s)
                yield
            st["aT"] = st["wT"] = done
            if L == 0:
                x1_ready[b] = t
            else:
                x1_ready[("out", u)] = done

        def drain(*gens):
            for g in gens:
                for _ in g:
                    pass

        ahead, behind = [], []
        credit = [0]

        def advance_ahead(ns):
            credit[0] += ns
            while credit[0] > 0 and ahead:
                try:
                    credit[0] -= next(ahead[0])
                except StopIteration:
                    ahead.pop(0)
            if not ahead:
                credit[0] = 0

        def advance_behind():
            while behind:
                try:
                    if next(behind[0][1]) is None:
                        return
                except StopIteration:
                    behind.pop(0)

        def complete(key):
            while any(k == key for k, _ in behind):
                advance_behind()

        for _ in split_x(0):
            pass
        w_ready["q0"] = split(wq, sq0, t_q0, lo=DV)
        drain(split_c(0))
        split_rest()
        constants()
        SP.wait(w_ready["q0"], w_ready["k0"], set_up["ind"])
        load512(wki1, Wki1, l_w["ip1"])
        w_ready["ip1"] = load512(wvi1, Wvi1, l_w["ip1"])
        drain(queries(0), keys(0))
        for g in range(NG):
            load_pack(0, g)
        load_ind(0)
        drain(split_x(1), values(0), ip_prep(), split_c(1))
        SP.wait(ip_read[0])
        t_w["o0"] = load_twice(so0, Wo0, l_w["o0"])
        ahead += [prepare(1), prepare(2)]
        late = 0
        for h in range(H):
            score_max(0, h)
            advance_ahead(900)
            if (1, "k") in st_done and late < NG:
                load_pack(1, late)
                late += 1
        shift_rows(0)
        advance_ahead(6000)
        while late < NG:
            load_pack(1, late)
            late += 1
        load_ind(1)
        scores(0, 0)
        scores(0, 1)

        def weigh_behind(u, g):
            evacuate(u, g)
            behind.append(((u, g), normalize(u, g)))
            if g == NG - 1:
                if u == B:
                    behind.append((("ip", u), ip_values(u)))
                behind.append((("end", u), finish(u)))

        maxed = [H]

        def maxima(u, h, mh, lead, rate):
            unit, head = divmod(maxed[0], H)
            goal = (u + 2) * H + max(0, h + 1 + lead - H) if h >= mh else min((u + 2) * H, (u + 1) * H + lead + (rate * (h + 1) + 3) // 4)
            if maxed[0] < goal and (unit, head // 4) in ld_done:
                score_max(unit, head)
                maxed[0] += 1

        for u in range(U):
            step[0] = u
            if u and u + 2 < U:
                ahead.append(prepare(u + 2))
            loads = 0
            mh, lead, rate = MH[u >= B], LEAD[u >= B], RATE[u >= B]
            early, late = EARLY[u >= B - 2], LATE[u >= B - 2]
            for h in range(H):
                if h == mh and u + 1 < U:
                    while maxed[0] < (u + 2) * H:
                        score_max(*divmod(maxed[0], H))
                        maxed[0] += 1
                    shift_rows(u + 1)
                before = divmod(u * NG + h // 4 - 1, NG) if h % 4 == 0 and u * NG + h // 4 else None
                maxima(u, h, mh, lead, rate)
                if h == 8 and u > B:
                    behind.append((("ip", u), ip_values(u)))
                if u == 0 and h == 6:
                    w_ready["o0"] = split(wo, so0, t_w["o0"])
                if u == 1 and h == 6:
                    SP.wait(w_ready["o0"])
                    t_w["q1"] = load_twice(sq1, Wq1, l_w["q1"])
                    t_w["k1"] = load512(sk1, Wk1, l_w["k1"])
                if h == 2 and u + 3 < U and u + 3 != B + 4:
                    load_ctx(u + 3)
                advance_behind()
                advance_ahead(late if h >= TURN else early)
                if u >= B:
                    quad(u, h)
                if before:
                    s = u * NG + h // 4 - 3
                    complete((s // NG, s % NG))
                    weigh(*before)
                advance_behind()
                if u >= B:
                    quad_y(u, h)
                if before and EARLY_EVAC[u >= B]:
                    weigh_behind(*before)
                if u * H + h + 2 < U * H:
                    scores(*divmod(u * H + h + 2, H))
                if before and not EARLY_EVAC[u >= B]:
                    weigh_behind(*before)
                maxima(u, h, mh, lead, rate)
                advance_ahead(late if h >= TURN else early)
                if h >= LH and (u + 2, "k") in st_done and loads < NG and (u, loads) in s2_done:
                    load_pack(u + 2, loads)
                    loads += 1
            if u + 2 < U:
                drain(*ahead)
                ahead.clear()
                while loads < NG:
                    load_pack(u + 2, loads)
                    loads += 1
                if u + 2 in (B, B + 1):
                    load_ind(u + 2)
        weigh(U - 1, NG - 1)
        weigh_behind(U - 1, NG - 1)
        while behind:
            advance_behind()
        SP.wait(l_out.all())
        for land in list(l_w.values()) + l_x + [l_c]:
            SP.wait(land.all())

        block = ctx.enter_context(nc.Block())
        block.tensor(PE.run)
        block.scalar(AC.run)
        block.vector(DV.run)
        block.sync(SP.run)
        block.gpsimd(PO.run)


def kernel(**inputs):
    import numpy as _np
    import concourse.bacc as _bacc
    from concourse import mybir as _mybir
    from concourse.bass_utils import run_bass_kernel_spmd as _run

    g = {k: _np.asarray(v) for k, v in inputs.items()}
    T = lambda a: _np.ascontiguousarray(a.T)

    def col(v):
        out = _np.zeros((3, 128), v.dtype)
        out[0], out[1], out[2, :64] = v[0:128], v[128:256], v[256:320]
        return T(out)

    ctx = g["ctx_2048"]
    ind = _np.zeros((4, 2, KT), _np.float32)
    ind[0:2, 0, 0:TXT0] = -1.0
    ind[2:4, 0, TXT0:S] = -1.0
    ind[0:2, 1, NIP:S] = -1.0
    ind[2, 1, S:KT] = -1.0
    hm = _np.zeros((128, 3, H), _np.float32)
    for c in range(C):
        hm[c % 128, c // 128, c // D] = 1.0
    arrays = {
        "xT": T(g["x"].reshape(B * S, C)),
        "cT": T(ctx.reshape(B * S, E)),
        "cipT": T(ctx[:, TXT1:, :].reshape(B * NIP, E)),
        "fs": T(g["fside_S_0"].reshape(2, 128)),
        "Wq0": T(g["L0_xattn_Wq"]), "Wk0": T(g["L0_xattn_Wk"]), "Wv0": T(g["L0_xattn_Wv"]),
        "Wki0": T(g["L0_xattn_Wk_ip"]), "Wvi0": T(g["L0_xattn_Wv_ip"]), "Wo0": T(g["L0_xattn_Wo"]),
        "bo0": col(g["L0_xattn_bo"]),
        "Wq1": g["L1_xattn_W_q"], "Wk1": g["L1_xattn_W_k"], "Wv1": g["L1_xattn_W_v"],
        "Wki1": g["L1_xattn_W_k_ip"], "Wvi1": g["L1_xattn_W_v_ip"], "Wo1": g["L1_xattn_W_out"],
        "bo1": col(g["L1_xattn_b_out"]),
        "ident": _np.eye(128, dtype=_np.float32), "ind": ind, "hm": hm,
    }
    nc = _bacc.Bacc("TRN2", target_bir_lowering=False, num_devices=1, dynamic_dma_scratch_size=1024)
    args, feeds = [], {}
    for name, a in arrays.items():
        a = _np.ascontiguousarray(a)
        feeds[f"in_{name}"] = a
        args.append(nc.dram_tensor(f"in_{name}", a.shape, _mybir.dt.from_np(a.dtype), kind="ExternalInput").ap())
    args.append(nc.dram_tensor("out_T", (C, B * S), _mybir.dt.float32, kind="ExternalOutput").ap())
    build(nc, *args)
    r = _run(nc, [feeds], core_ids=[0])
    got = r.results[0]["out_T"]
    return _np.ascontiguousarray(got.T).reshape(B, S, C)
```
